# Optimizing a Trainium2 kernel written in Bass

```python
import numpy as np
import jax
import jax.numpy as jnp

def _softmax(x, axis=-1):
    return jax.nn.softmax(x, axis=axis)

def _gelu(x):
    return jax.nn.gelu(x, approximate=True)

def _silu(x):
    return jax.nn.silu(x)

def _sigmoid(x):
    return jax.nn.sigmoid(x)

def _layernorm(x, axis=-1, eps=1e-05):
    m = jnp.mean(x, axis=axis, keepdims=True)
    v = jnp.var(x, axis=axis, keepdims=True)
    return (x - m) / jnp.sqrt(v + eps)

def _scatter_add(tgt, idx, src, axis=0):
    return tgt.at[idx].add(src)

def _segment_sum(src, seg, n):
    return jax.ops.segment_sum(src, seg, n)
kernel_name = 'mk_gnn_preln_d1_gnn_r8_3e21d9'

def setup_inputs(seed: int=0):
    np.random.seed(seed)
    _w = jnp.asarray

    def _rec_inputs():
        import jax
        import jax.numpy as jnp
        _gk = jax.random.key(seed)
        x = -8.776e-05 + 1 * jax.random.normal(jax.random.fold_in(_gk, 1), (12500, 256), jnp.float32)
        _s = jax.random.randint(jax.random.fold_in(_gk, 2), (100000,), 0, 12500, jnp.int32)
        _d = jax.random.randint(jax.random.fold_in(_gk, 3), (100000,), 0, 12500, jnp.int32)
        _loop = jnp.arange(12500, dtype=jnp.int32)
        src = jnp.concatenate([_s, _d, _loop])
        dst = jnp.concatenate([_d, _s, _loop])
        _o = jnp.argsort(dst, stable=True)
        src = src[_o]
        dst = dst[_o]
        edge_attr_64 = jax.random.uniform(jax.random.fold_in(_gk, 11), (212500, 64), jnp.float32, 0.0, 1)
        edge_weight = jax.random.uniform(jax.random.fold_in(_gk, 13), (212500,), jnp.float32, 0.0, 0.999995)
        return (x, src, dst, edge_attr_64, edge_weight)
    x, src, dst, edge_attr_64, edge_weight = _rec_inputs()

    def _L0_gnn_setup():
        import jax, jax.numpy as jnp
        import numpy as np
        N = 2500
        E = 30000
        H = 256
        NH = 8
        HD = H // NH
        NRBF = 64
        EPS = 1e-05
        key = jax.random.key(seed)
        ks = jax.random.split(key, 20)
        s = 0.05
        return {'x': jax.random.normal(ks[0], (N, H), jnp.float32), 'edge_index': jax.random.randint(ks[1], (2, E), 0, N, dtype=jnp.int64), 'rbf': jax.random.uniform(ks[2], (E, NRBF), jnp.float32), 'cutoff': jax.random.uniform(ks[3], (E,), jnp.float32), 'w1': jax.random.normal(ks[4], (NRBF, H), jnp.float32) * s, 'b1': jnp.zeros((H,), jnp.float32), 'w2': jax.random.normal(ks[5], (H, H), jnp.float32) * s, 'b2': jnp.zeros((H,), jnp.float32), 'ln_w': jnp.ones((H,), jnp.float32), 'ln_b': jnp.zeros((H,), jnp.float32), 'wq': jax.random.normal(ks[6], (H, H), jnp.float32) * s, 'bq': jnp.zeros((H,), jnp.float32), 'wk': jax.random.normal(ks[7], (H, H), jnp.float32) * s, 'bk': jnp.zeros((H,), jnp.float32), 'wv': jax.random.normal(ks[8], (H, H), jnp.float32) * s, 'bv': jnp.zeros((H,), jnp.float32), 'wo': jax.random.normal(ks[9], (H, H), jnp.float32) * s, 'bo': jnp.zeros((H,), jnp.float32), 'gate': jnp.array([0.1], jnp.float32)}
    _L0_gnn_all = _L0_gnn_setup()
    _L0_gnn_in = {k: v for k, v in _L0_gnn_all.items() if k in ('w1', 'b1', 'w2', 'b2', 'ln_w', 'ln_b', 'wq', 'bq', 'wk', 'bk', 'wv', 'bv', 'wo', 'bo', 'gate')}
    del _L0_gnn_all
    return {'x': x, 'src': src, 'dst': dst, 'edge_attr_64': edge_attr_64, 'edge_weight': edge_weight, 'L0_gnn_w1': _L0_gnn_in['w1'], 'L0_gnn_b1': _L0_gnn_in['b1'], 'L0_gnn_w2': _L0_gnn_in['w2'], 'L0_gnn_b2': _L0_gnn_in['b2'], 'L0_gnn_ln_w': _L0_gnn_in['ln_w'], 'L0_gnn_ln_b': _L0_gnn_in['ln_b'], 'L0_gnn_wq': _L0_gnn_in['wq'], 'L0_gnn_bq': _L0_gnn_in['bq'], 'L0_gnn_wk': _L0_gnn_in['wk'], 'L0_gnn_bk': _L0_gnn_in['bk'], 'L0_gnn_wv': _L0_gnn_in['wv'], 'L0_gnn_bv': _L0_gnn_in['bv'], 'L0_gnn_wo': _L0_gnn_in['wo'], 'L0_gnn_bo': _L0_gnn_in['bo'], 'L0_gnn_gate': _L0_gnn_in['gate']}

def reference(x, src, dst, edge_attr_64, edge_weight, L0_gnn_w1, L0_gnn_b1, L0_gnn_w2, L0_gnn_b2, L0_gnn_ln_w, L0_gnn_ln_b, L0_gnn_wq, L0_gnn_bq, L0_gnn_wk, L0_gnn_bk, L0_gnn_wv, L0_gnn_bv, L0_gnn_wo, L0_gnn_bo, L0_gnn_gate):
    import jax
    import jax.numpy as jnp

    def _L0_gnn_ref(x, edge_index, rbf, cutoff, w1, b1, w2, b2, ln_w, ln_b, wq, bq, wk, bk, wv, bv, wo, bo, gate):
        import jax, jax.numpy as jnp
        import numpy as np
        N = 2500
        E = 30000
        H = 256
        NH = 8
        HD = H // NH
        NRBF = 64
        EPS = 1e-05
        row, col = (edge_index[0], edge_index[1])
        n = x.shape[0]
        mu = jnp.mean(x, axis=-1, keepdims=True)
        var = jnp.mean((x - mu) ** 2, axis=-1, keepdims=True)
        xn = (x - mu) * jax.lax.rsqrt(var + EPS) * ln_w + ln_b
        w_phys = (jax.nn.silu(rbf @ w1 + b1) @ w2 + b2) * cutoff[:, None]
        msg_phys = xn[col] * w_phys
        Q = (xn @ wq + bq).reshape(n, NH, HD)
        K = (xn @ wk + bk).reshape(n, NH, HD)
        V = (xn @ wv + bv).reshape(n, NH, HD)
        q_e, k_e, v_e = (Q[row], K[col], V[col])
        scores = jnp.sum(q_e * k_e, axis=-1) / np.sqrt(HD)
        scores = scores * cutoff[:, None]
        attn = jax.nn.softmax(scores, axis=1)
        msg_attn = (attn[..., None] * v_e).reshape(-1, H)
        combined = msg_phys + gate * msg_attn
        aggr = jax.ops.segment_sum(combined, row, num_segments=n)
        return x + aggr @ wo + bo
    edge_index = jnp.stack([src, dst])
    h = jnp.maximum(_layernorm(x, axis=-1), 0.0)
    x = x + _L0_gnn_ref(h, edge_index, edge_attr_64, edge_weight, L0_gnn_w1, L0_gnn_b1, L0_gnn_w2, L0_gnn_b2, L0_gnn_ln_w, L0_gnn_ln_b, L0_gnn_wq, L0_gnn_bq, L0_gnn_wk, L0_gnn_bk, L0_gnn_wv, L0_gnn_bv, L0_gnn_wo, L0_gnn_bo, L0_gnn_gate)
    return x

_drawn_inputs = setup_inputs


def setup_inputs(seed=0):
    import zlib

    import numpy as np

    out = dict(_drawn_inputs(seed))
    spreads = {'L0_gnn_b1': (0.0, 0.1),
     'L0_gnn_b2': (0.0, 0.1),
     'L0_gnn_ln_w': (1.0, 0.2),
     'L0_gnn_ln_b': (0.0, 0.1),
     'L0_gnn_bq': (0.0, 2.0),
     'L0_gnn_bk': (0.0, 0.8),
     'L0_gnn_bv': (0.0, 0.742),
     'L0_gnn_bo': (0.0, 0.1)}
    factors = {'L0_gnn_wq': 6.642, 'L0_gnn_wk': 6.664}
    for name, (base, spread) in spreads.items():
        noise = np.random.default_rng([zlib.crc32(name.encode()), seed]).standard_normal(out[name].shape)
        drawn = base * np.exp(spread * noise) if base else spread * noise
        out[name] = jnp.asarray(drawn.astype(out[name].dtype))
    for name, factor in factors.items():
        out[name] = (out[name] * factor).astype(out[name].dtype)
    return out
```

```python
from contextlib import ExitStack

import concourse.bass as bass
from concourse import mybir

F32 = mybir.dt.float32
BF16 = mybir.dt.bfloat16
I32 = mybir.dt.int32
ALU = mybir.AluOpType
ACT = mybir.ActivationFunctionType
AX_X = mybir.AxisListType.X

P = 128
N = 12500
E = 212500
H = 256
NH, HD = 8, 32
NRBF = 64
EPS = 1e-5
BUCKETS = -(-N // P)
NPAD = BUCKETS * P
LAST_ROWS = N - (BUCKETS - 1) * P
COLS = E // P
TAIL = E - COLS * P
RCOLS = 4
RGROUPS = -(-(COLS + 1) // RCOLS)
CPAD = RGROUPS * RCOLS
NOBUCKET = 200
SCOLS = 10
SGROUPS = COLS // SCOLS
SHIFT = 7
UNIT = 2 * P
USHIFT = 8
DEPTH = 4
UNITS = -(-((E + BUCKETS * (UNIT - 1)) // UNIT) // DEPTH) * DEPTH
SLOTS = UNITS * UNIT
REC = NRBF + 4
R_ONE, R_W, R_DST, R_LOC = NRBF, NRBF + 1, NRBF + 2, NRBF + 3
TAB = 3 * H
NG = 7
NGROUPS = BUCKETS // NG
ZROWS = 16
ZPER = SLOTS // P


def build(nc, x, src, dst, rbf, weight, w1, b1, w2, b2, ln_w, ln_b, wq, bq, wk, bk, wv, bv, wo, bo, gate, out):
    recs = nc.dram_tensor("records", [SLOTS, REC], F32).ap()
    table = nc.dram_tensor("kvx_table", [NPAD, TAB], F32).ap()
    qparts = nc.dram_tensor("q_parts", [NPAD, 3 * H], BF16).ap()
    base = nc.dram_tensor("x_plus_h", [NPAD, H], F32).ap()
    with ExitStack() as ctx:
        def sb(name, shape, dt, stack=ctx):
            return stack.enter_context(nc.sbuf_tensor(name, shape, dt))

        def sem(name):
            return ctx.enter_context(nc.semaphore(name))

        ident = sb("ident", [P, P], F32)
        ones_bf = sb("ones_bf", [P, P], BF16)
        iota1 = sb("iota1", [P, P], F32)
        w1s = sb("w1s", [NRBF + 1, H], F32)
        w2s = sb("w2s", [P, 2, H], F32)
        wos = sb("wos", [P, 2, H], F32)
        bparts = sb("bparts", [3, 6 * H], BF16)
        unit_bucket = sb("unit_bucket", [1, UNITS], I32)
        BQ, BK, BV, B2, BO = (slice(k * H, (k + 1) * H) for k in (0, 1, 2, 3, 4))
        BKV = slice(H, 3 * H)

        prep(nc, ctx, sb, sem, x, src, dst, rbf, weight, w1, b1, w2, b2, ln_w, ln_b, wq, bq, wk, bk, wv, bv, wo, bo,
             gate, recs, table, qparts, base, ident, ones_bf, iota1, w1s, w2s, wos, bparts, unit_bucket, BQ, BKV)
        aggr = sb("aggr", [P, BUCKETS, H], F32)
        edges(nc, sb, sem, recs, table, qparts, ident, ones_bf, iota1, w1s, w2s, bparts, unit_bucket, aggr, B2)
        finish(nc, sb, sem, base, out, ident, ones_bf, wos, bparts, aggr, BO)


def prep(nc, ctx, sb_, sem, x, src, dst, rbf, weight, w1, b1, w2, b2, ln_w, ln_b, wq, bq, wk, bk, wv, bv, wo, bo,
         gate, recs, table, qparts, base, ident, ones_bf, iota1, w1s, w2s, wos, bparts, unit_bucket, BQ, BKV):
    with ExitStack() as st:
        def sb(name, shape, dt):
            return st.enter_context(nc.sbuf_tensor(name, shape, dt))

        def ps(name, shape, dt=F32):
            return st.enter_context(nc.psum_tensor(name, shape, dt))

        src_i = sb("src_i", [P, CPAD], I32)
        dst_i = sb("dst_i", [P, CPAD], I32)
        tmp_i = sb("tmp_i", [P, CPAD], I32)
        wgt = sb("wgt", [P, CPAD], F32)
        bucket = sb("bucket", [P, CPAD], BF16)
        meta = sb("meta", [P, CPAD, 4], F32)
        pos = sb("pos", [P, CPAD], F32)
        eq = sb("eq", [P, 2, CPAD], BF16)
        bucket_ids = sb("bucket_ids", [P, BUCKETS], F32)
        bucket_ids_bf = sb("bucket_ids_bf", [P, BUCKETS], BF16)
        tri = sb("tri", [P, P], BF16)
        ones_f = sb("ones_f", [P, P], F32)
        count = sb("count", [P, BUCKETS], F32)
        zero98 = sb("zero98", [P, BUCKETS], F32)
        units_i = sb("units_i", [P, BUCKETS], I32)
        units_f = sb("units_f", [P, BUCKETS], F32)
        end_f = sb("end_f", [P, BUCKETS], F32)
        end_col = sb("end_col", [BUCKETS, 1], F32)
        unit_no = sb("unit_no", [BUCKETS, UNITS], F32)
        past = sb("past", [BUCKETS, UNITS], F32)
        carry = sb("carry", [P, 2, BUCKETS], F32)
        onehot = sb("onehot", [P, 2, RCOLS, BUCKETS], BF16)
        ranked = sb("ranked", [P, 2, RCOLS, BUCKETS], F32)
        rec = sb("rec", [P, 2, SCOLS, REC], F32)
        slot_i = sb("slot_i", [P, 2, SCOLS], I32)
        tail_rec = sb("tail_rec", [P, REC], F32)
        tail_slot = sb("tail_slot", [P, 1], I32)
        zero = sb("zero", [P, ZROWS * REC], F32)
        bias_f = sb("bias_f", [3, 6 * H], F32)
        bias_r = sb("bias_r", [3, 6 * H], F32)
        bias_p = sb("bias_p", [3, 3, 6 * H], BF16)
        w2raw = sb("w2raw", [P, 2, H], F32)
        wqs = sb("wqs", [P, 2, H], F32)
        wkvs = sb("wkvs", [P, 2, 2 * H], F32)
        lnw_b = sb("lnw_b", [P, H], F32)
        lnb_b = sb("lnb_b", [P, H], F32)
        gate_b = sb("gate_b", [P, 1], F32)
        xg = sb("xg", [P, 2, NG, H], F32)
        hg = sb("hg", [P, NG, H], F32)
        stats = sb("stats", [P, NG, 6], F32)
        mv = sb("mv", [P, 2, NG, 2], F32)
        ve = sb("ve", [P, 2, NG], F32)
        sd = sb("sd", [P, 2, NG], F32)
        rs = sb("rs", [P, 2, NG], F32)
        r2 = sb("r2", [P, 2, NG], F32)
        nb = sb("nb", [P, 2, NG], F32)
        kvx = sb("kvx", [P, NG, TAB], F32)
        qf = sb("qf", [P, NG, H], F32)
        qr = sb("qr", [P, NG, H], F32)
        q3 = sb("q3", [P, NG, 3, H], BF16)
        xnT = sb("xnT", [P, 2, 2, P], F32)

        rank_ps = ps("rank_ps", [P, 2, 512])
        setup_ps = ps("setup_ps", [P, 2, 512])
        t_ps = ps("t_ps", [P, 2, P])
        t_ps_pad = ps("t_ps_pad", [P, 256])
        kv_ps = ps("kv_ps", [P, 512])
        q_ps = ps("q_ps", [P, 512])

        s = {n: sem("a_" + n) for n in (
            "edges_loaded", "params_loaded", "filled", "consts", "v", "pe_setup", "dve_setup", "onehot_ready",
            "carry_ready", "ranks_ready", "ranks_picked", "positions_ready", "stored", "zeros_stored", "stats_waited", "placed_waited",
            "placed", "loaded_tail", "tail_stored",
            "x_loaded0", "x_loaded1", "stats_done", "aggregated", "ve_done", "sd_done", "small", "bias_done",
            "h_done", "base_done", "base_stored", "z_done", "lnw_done", "xn_done", "xnt_ps", "xnt_sb", "kv_done", "q_done", "kv_out", "q_out",
            "q_hi", "q_rest", "q_mid", "q_lo", "table_stored", "q_stored")}
        rec_loaded = [sem(f"a_rec_loaded{q}") for q in range(2)]
        scattered = [sem(f"a_scattered{q}") for q in range(2)]

        rbf_v = rbf[0:COLS * P, :].rearrange("(p t) f -> p t f", p=P)
        rec_v = recs.rearrange("(p s) f -> p (s f)", p=P)
        NEDGE = 16 * 6
        NPAR = 16 * 16

        block = st.enter_context(nc.Block())

        @block.sync
        def _(sp):
            sp.wait_ge(s["filled"], 3)
            for to, of in ((src_i, src), (dst_i, dst), (wgt, weight)):
                sp.dma_start(to[:, 0:COLS], of[0:COLS * P].rearrange("(p t) -> p t", p=P)).then_inc(s["edges_loaded"], 16)
                sp.dma_start(to[0:TAIL, COLS:COLS + 1], of[COLS * P:E].rearrange("(p t) -> p t", t=1)).then_inc(s["edges_loaded"], 16)
            for to, of in ((w1s[0:NRBF, :], w1), (w1s[NRBF:NRBF + 1, :], b1.rearrange("(a n) -> a n", a=1)),
                           (w2raw[:], w2.rearrange("(c p) n -> p c n", p=P)), (wos[:], wo.rearrange("(c p) n -> p c n", p=P)),
                           (wqs[:], wq.rearrange("(c p) n -> p c n", p=P)),
                           (wkvs[:, :, 0:H], wk.rearrange("(c p) n -> p c n", p=P)),
                           (wkvs[:, :, H:2 * H], wv.rearrange("(c p) n -> p c n", p=P)),
                           (lnw_b[:], ln_w.partition_broadcast(P)), (lnb_b[:], ln_b.partition_broadcast(P)),
                           (gate_b[:], gate.partition_broadcast(P)),
                           (bias_f[:, 0:H], bq.partition_broadcast(3)), (bias_f[:, H:2 * H], bk.partition_broadcast(3)),
                           (bias_f[:, 2 * H:3 * H], bv.partition_broadcast(3)), (bias_f[:, 3 * H:4 * H], b2.partition_broadcast(3)),
                           (bias_f[:, 4 * H:5 * H], bo.partition_broadcast(3)), (bias_f[:, 5 * H:6 * H], bo.partition_broadcast(3))):
                sp.dma_start(to, of).then_inc(s["params_loaded"], 16)
            sp.wait_ge(s["consts"], 1)
            for k in range(0, ZPER, 8 * ZROWS):
                n = min(8 * ZROWS, ZPER - k) // ZROWS
                sp.dma_start(rec_v[:, k * REC:(k + n * ZROWS) * REC].rearrange("p (n f) -> p n f", n=n),
                             zero[:, :].unsqueeze(1).to_broadcast([P, n, ZROWS * REC])).then_inc(s["zeros_stored"], 16)
            sp.dma_start(tail_rec[0:TAIL, 0:NRBF], rbf[COLS * P:E, :]).then_inc(s["loaded_tail"], 16)
            for q in range(2):
                sp.dma_start(rec[:, q, :, 0:NRBF], rbf_v[:, q * SCOLS:(q + 1) * SCOLS, :]).then_inc(rec_loaded[q], 16)
            with sp.Fori(1, SGROUPS // 2) as i:
                for q in range(2):
                    sp.wait_ge(scattered[q], i * (16 * SCOLS))
                    sp.dma_start(rec[:, q, :, 0:NRBF], rbf_v[:, bass.ds((2 * i + q) * SCOLS, SCOLS), :]).then_inc(rec_loaded[q], 16)

        @block.gpsimd
        def _(pool):
            pool.memset(src_i[:, COLS:CPAD], NOBUCKET << SHIFT).then_inc(s["filled"], 1)
            pool.memset(dst_i[:, COLS:CPAD], 0).then_inc(s["filled"], 1)
            pool.memset(wgt[:, COLS:CPAD], 0.0).then_inc(s["filled"], 1)
            pool.memset(zero[:, :], 0.0).then_inc(s["consts"], 1)
            pool.memset(ident[:, :], 0.0).then_inc(s["consts"], 1)
            pool.memset(ones_bf[:, :], 1.0).then_inc(s["consts"], 1)
            pool.memset(ones_f[:, :], 1.0).then_inc(s["consts"], 1)
            pool.memset(zero98[:, :], 0.0).then_inc(s["consts"], 1)
            pool.iota(iota1[:, :], [[1, P]], base=1, channel_multiplier=0, allow_small_or_imprecise_dtypes=True).then_inc(s["consts"], 1)
            pool.iota(bucket_ids[:, :], [[1, BUCKETS]], base=0, channel_multiplier=0, allow_small_or_imprecise_dtypes=True).then_inc(s["consts"], 1)
            pool.iota(unit_no[:, :], [[1, UNITS]], base=0, channel_multiplier=0, allow_small_or_imprecise_dtypes=True).then_inc(s["consts"], 1)
            pool.wait_ge(s["consts"], 8)
            pool.affine_select(out=ident[:, :], in_=ident[:, :], compare_op=ALU.not_equal, fill=1.0, base=0,
                               pattern=[[-1, P]], channel_multiplier=1).then_inc(s["consts"], 1)
            pool.affine_select(out=tri[:, :], in_=ones_bf[:, :], compare_op=ALU.is_gt, fill=0.0, base=0,
                               pattern=[[1, P]], channel_multiplier=-1).then_inc(s["consts"], 1)
            pool.wait_ge(s["zeros_stored"], 16 * -(-ZPER // (8 * ZROWS)))
            with pool.Fori(0, SGROUPS // 2) as i:
                for q in range(2):
                    pool.wait_ge(rec_loaded[q], i * 16 + 16)
                    pool.wait_ge(s["positions_ready"], i * (2 * SCOLS // RCOLS) + -(-(q + 1) * SCOLS // RCOLS))
                    pool.tensor_copy(rec[:, q, :, NRBF:REC], meta[:, bass.ds((2 * i + q) * SCOLS, SCOLS), :]).then_inc(s["placed"], 1)
                    pool.tensor_copy(slot_i[:, q, :], pos[:, bass.ds((2 * i + q) * SCOLS, SCOLS)]).then_inc(s["placed"], 1)
                    pool.wait_ge(s["placed"], i * 4 + 2 * q + 2)
                    pool.sem_inc(s["placed_waited"], 1)
                    for t in range(SCOLS):
                        pool.indirect_dma_start(recs, bass.IndirectOffsetOnAxis(ap=slot_i[:, q, t:t + 1], axis=0),
                                                rec[:, q, t, :], None).then_inc(scattered[q], 16)
            pool.wait_ge(s["positions_ready"], RGROUPS)
            pool.wait_ge(s["loaded_tail"], 16)
            pool.tensor_copy(tail_rec[0:TAIL, NRBF:REC], meta[0:TAIL, COLS, :]).then_inc(s["placed"], 1)
            pool.tensor_copy(tail_slot[0:TAIL, :], pos[0:TAIL, COLS:COLS + 1]).then_inc(s["placed"], 1)
            pool.wait_ge(s["placed"], 2 * SGROUPS + 2)
            pool.indirect_dma_start(recs, bass.IndirectOffsetOnAxis(ap=tail_slot[0:TAIL, :], axis=0),
                                    tail_rec[0:TAIL, :], None).then_inc(s["tail_stored"], 16)
            pool.wait_ge(s["tail_stored"], 16)
            for q in range(2):
                pool.wait_ge(scattered[q], 16 * SCOLS * SGROUPS // 2)

        @block.vector
        def _(dve):
            steps = [0]

            def link(ins):
                steps[0] += 1
                ins.then_inc(s["v"], 1)
                dve.wait_ge(s["v"], steps[0])

            dve.wait_ge(s["edges_loaded"], NEDGE)
            dve.wait_ge(s["consts"], 10)
            dve.tensor_copy(bucket_ids_bf[:], bucket_ids[:])
            dve.tensor_copy(meta[:, :, 1], wgt[:])
            dve.tensor_copy(meta[:, :, 2], dst_i[:])
            dve.memset(meta[:, :, 0], 1.0)
            link(dve.tensor_scalar(tmp_i[:], src_i[:], SHIFT, None, ALU.logical_shift_right))
            link(dve.tensor_copy(bucket[:], tmp_i[:]))
            link(dve.tensor_scalar(tmp_i[:], src_i[:], P - 1, None, ALU.bitwise_and))
            link(dve.tensor_scalar(meta[:, :, 3], tmp_i[:], 1.0, None, ALU.add))
            def tally(b, q):
                dve.tensor_scalar(eq[:, q, :], bucket[:], bucket_ids[:, bass.ds(b, 1)], 0.0, ALU.is_equal, ALU.add,
                                  accum_out=count[:, bass.ds(b, 1)]).then_inc(s["dve_setup"], 1)
            tally(0, 0)
            tally(1, 1)
            with dve.Fori(1, BUCKETS // 2) as i:
                for q in range(2):
                    dve.wait_ge(s["dve_setup"], i * 2 + q - 1)
                    tally(i * 2 + q, q)
            dve.wait_ge(s["pe_setup"], 1)
            link(dve.tensor_scalar(units_i[:], setup_ps[:, 0, 0:BUCKETS], float(UNIT - 1), None, ALU.add))
            link(dve.tensor_scalar(units_i[:], units_i[:], USHIFT, None, ALU.logical_shift_right))
            link(dve.tensor_copy(units_f[:], units_i[:]))
            link(dve.tensor_tensor_scan(end_f[:], units_f[:], zero98[:], 0.0, ALU.add, ALU.add))
            link(dve.tensor_tensor(units_f[:], end_f[:], units_f[:], ALU.subtract))
            dve.tensor_scalar(carry[:, 0, :], units_f[:], float(UNIT), None, ALU.mult).then_inc(s["carry_ready"], 1)

            def make_onehot(g, q):
                dve.tensor_tensor(onehot[:, q, :, :], bucket[:, bass.ds(g * RCOLS, RCOLS)].unsqueeze(2).to_broadcast([P, RCOLS, BUCKETS]),
                                  bucket_ids_bf[:].unsqueeze(1).to_broadcast([P, RCOLS, BUCKETS]), ALU.is_equal).then_inc(s["onehot_ready"], 1)

            def pick_ranks(g, q):
                r = rank_ps[:, q, 0:(RCOLS + 1) * BUCKETS].rearrange("p (j b) -> p j b", b=BUCKETS)
                dve.wait_ge(s["ranks_ready"], g + 1)
                dve.tensor_copy(carry[:, 1 - q, :], r[:, RCOLS, :]).then_inc(s["carry_ready"], 1)
                dve.tensor_tensor(ranked[:, q, :, :], r[:, 0:RCOLS, :], onehot[:, q, :, :], ALU.mult).then_inc(s["ranks_picked"], 1)
                dve.wait_ge(s["ranks_picked"], g + 1)
                dve.tensor_reduce(pos[:, bass.ds(g * RCOLS, RCOLS)], ranked[:, q, :, :], AX_X, ALU.add).then_inc(s["positions_ready"], 1)

            make_onehot(0, 0)
            with dve.Fori(0, RGROUPS // 2 - 1) as i:
                make_onehot(i * 2 + 1, 1)
                pick_ranks(i * 2, 0)
                make_onehot(i * 2 + 2, 0)
                pick_ranks(i * 2 + 1, 1)
            make_onehot(RGROUPS - 1, 1)
            pick_ranks(RGROUPS - 2, 0)
            pick_ranks(RGROUPS - 1, 1)

            dve.wait_ge(s["pe_setup"], 2)
            link(dve.tensor_copy(end_col[:], setup_ps[0:BUCKETS, 1, 0:1]))
            dve.tensor_scalar(past[:], unit_no[:], end_col[:, 0:1], None, ALU.is_ge).then_inc(s["dve_setup"], 1)
            HU = UNITS // 2
            dve.wait_ge(s["pe_setup"], 3)
            for k in range(2):
                dve.tensor_scalar(unit_bucket[:, k * HU:(k + 1) * HU], setup_ps[0:1, k, 0:HU], float(BUCKETS - 1), None, ALU.min)

            dve.wait_ge(s["params_loaded"], NPAR)
            dve.tensor_scalar(w2s[:], w2raw[:], 0.5, None, ALU.mult)
            link(dve.tensor_copy(bias_p[:, 0, :], bias_f[:]))
            link(dve.tensor_tensor(bias_r[:], bias_f[:], bias_p[:, 0, :], ALU.subtract))
            link(dve.tensor_copy(bias_p[:, 1, :], bias_r[:]))
            link(dve.tensor_tensor(bias_p[:, 2, :], bias_r[:], bias_p[:, 1, :], ALU.subtract))
            link(dve.tensor_scalar(bias_f[:], bias_p[:, 0, :], ident[0:3, 0:1], None, ALU.mult))
            link(dve.scalar_tensor_tensor(bias_r[:], bias_p[:, 1, :], ident[0:3, 1:2], bias_f[:], ALU.mult, ALU.add))
            dve.scalar_tensor_tensor(bparts[:], bias_p[:, 2, :], ident[0:3, 2:3], bias_r[:], ALU.mult, ALU.add).then_inc(s["bias_done"], 1)

            def normaliser(g, k, first):
                c = g * 2 + k
                dve.wait_ge(s["aggregated"], c * NG + NG)
                dve.tensor_scalar(ve[:, k, :], mv[:, k, :, 1], EPS, None, ALU.add).then_inc(s["ve_done"], 1)
                dve.wait_ge(s["sd_done"], c + 1)
                dve.reciprocal(rs[:, k, :], sd[:, k, :]).then_inc(s["small"], 1)
                dve.wait_ge(s["small"], c * 6 + 1)
                dve.tensor_tensor(r2[:, k, :], rs[:, k, :], rs[:, k, :], ALU.mult).then_inc(s["small"], 1)
                dve.wait_ge(s["small"], c * 6 + 2)
                dve.tensor_tensor(r2[:, k, :], r2[:, k, :], ve[:, k, :], ALU.mult).then_inc(s["small"], 1)
                dve.wait_ge(s["small"], c * 6 + 3)
                dve.tensor_scalar(r2[:, k, :], r2[:, k, :], -0.5, 1.5, ALU.mult, ALU.add).then_inc(s["small"], 1)
                dve.wait_ge(s["small"], c * 6 + 4)
                dve.tensor_tensor(rs[:, k, :], rs[:, k, :], r2[:, k, :], ALU.mult).then_inc(s["small"], 1)
                dve.wait_ge(s["small"], c * 6 + 5)
                dve.scalar_tensor_tensor(nb[:, k, :], mv[:, k, :, 0], -1.0, rs[:, k, :], ALU.mult, ALU.mult).then_inc(s["small"], 1)

            def statistics(of, k, c):
                for t in range(NG):
                    dve.bn_stats(stats[:, t, :], of[:, t, :]).then_inc(s["stats_done"], 1)
                dve.wait_ge(s["stats_done"], c * NG + NG)
                dve.sem_inc(s["stats_waited"], 1)
                for t in range(NG):
                    dve.bn_aggr(mv[:, k, t, :], stats[:, t, :]).then_inc(s["aggregated"], 1)

            def nodes(g, q, i):
                dve.wait_ge(s[f"x_loaded{q}"], i * 32 + 32)
                statistics(xg[:, q], 0, g * 2)
                normaliser(g, 0, False)
                dve.wait_ge(s["h_done"], g * NG + NG)
                statistics(hg, 1, g * 2 + 1)
                normaliser(g, 1, False)
                dve.tensor_tensor(xg[:, q], xg[:, q], hg[:], ALU.add).then_inc(s["base_done"], 1)
                dve.wait_ge(s["z_done"], g * NG + NG)
                dve.tensor_tensor(hg[:], hg[:], lnw_b[:].unsqueeze(1).to_broadcast([P, NG, H]), ALU.mult).then_inc(s["lnw_done"], 1)
                dve.wait_ge(s["lnw_done"], g + 1)
                return None

            def xn_of(g):
                dve.tensor_tensor(kvx[:, :, 2 * H:3 * H], hg[:], lnb_b[:].unsqueeze(1).to_broadcast([P, NG, H]), ALU.add).then_inc(s["xn_done"], 1)

            def split_q(g):
                dve.wait_ge(s["q_hi"], g * NG + NG)
                dve.tensor_tensor(qr[:], qf[:], q3[:, :, 0, :], ALU.subtract).then_inc(s["q_rest"], 1)
                dve.wait_ge(s["q_rest"], g + 1)
                dve.tensor_copy(q3[:, :, 1, :], qr[:]).then_inc(s["q_mid"], 1)
                dve.wait_ge(s["q_mid"], g + 1)
                dve.tensor_tensor(q3[:, :, 2, :], qr[:], q3[:, :, 1, :], ALU.subtract).then_inc(s["q_lo"], 1)

            nodes(0, 0, 0)
            xn_of(0)
            split_q(0)
            nodes(1, 1, 0)
            dve.wait_ge(s["table_stored"], 16)
            xn_of(1)
            split_q(1)
            with dve.Fori(1, NGROUPS // 2) as i:
                for q in range(2):
                    nodes(i * 2 + q, q, i)
                    dve.wait_ge(s["table_stored"], i * 32 + 16 * q)
                    xn_of(i * 2 + q)
                    split_q(i * 2 + q)

        @block.tensor
        def _(pe):
            pe.wait_ge(s["dve_setup"], BUCKETS)
            pe.wait_ge(s["consts"], 10)
            pe.matmul(setup_ps[:, 0, 0:BUCKETS], ones_f[:], count[:], start=True, stop=True).then_inc(s["pe_setup"], 1)
            pe.wait_ge(s["carry_ready"], 1)
            pe.transpose(setup_ps[0:BUCKETS, 1, 0:P], end_f[:], ident[:]).then_inc(s["pe_setup"], 1)

            def rank(g, q, reused):
                r = rank_ps[:, q, 0:(RCOLS + 1) * BUCKETS].rearrange("p (j b) -> p j b", b=BUCKETS)
                pe.wait_ge(s["onehot_ready"], g + 1)
                if reused:
                    pe.wait_ge(s["ranks_picked"], g - 1)
                pe.wait_ge(s["carry_ready"], g + 1)
                pe.matmul(r, ident[:], carry[:, q, :].unsqueeze(1).to_broadcast([P, RCOLS + 1, BUCKETS]), start=True, stop=False)
                pe.matmul(r[:, 0:RCOLS, :], tri[:], onehot[:, q, :, :], start=False, stop=False)
                for j in range(RCOLS):
                    n = RCOLS - j
                    m = pe.matmul(r[:, j + 1:RCOLS + 1, :], ones_bf[:], onehot[:, q, j, :].unsqueeze(1).to_broadcast([P, n, BUCKETS]),
                                  start=False, stop=(n == 1))
                m.then_inc(s["ranks_ready"], 1)

            rank(0, 0, False)
            rank(1, 1, False)
            with pe.Fori(1, RGROUPS // 2) as i:
                rank(i * 2, 0, True)
                rank(i * 2 + 1, 1, True)
            HU = UNITS // 2
            pe.wait_ge(s["dve_setup"], BUCKETS + 1)
            for k in range(2):
                m = pe.matmul(setup_ps[0:1, k, 0:HU], ones_f[0:BUCKETS, 0:1], past[:, k * HU:(k + 1) * HU], start=True, stop=True)
            m.then_inc(s["pe_setup"], 1)

            pe.wait_ge(s["bias_done"], 1)
            pe.wait_ge(s["params_loaded"], NPAR)

            def node_tile(c, g, t, first):
                pe.wait_ge(s["xn_done"], g + 1)
                if not first:
                    pe.wait_ge(s["xnt_sb"], c)
                for k in range(2):
                    m = pe.transpose(t_ps[:, k, :], kvx[:, t, 2 * H + k * P:2 * H + (k + 1) * P], ident[:])
                m.then_inc(s["xnt_ps"], 1)
                pe.wait_ge(s["xnt_sb"], c + 1)
                if not first:
                    pe.wait_ge(s["kv_out"], c)
                pe.matmul(kv_ps[:, 0:2 * H], ones_bf[0:3, :], bparts[:, BKV], start=True, stop=False)
                for k in range(2):
                    m = pe.matmul(kv_ps[:, 0:2 * H], xnT[:, 0, k, :], wkvs[:, k, :], start=False, stop=(k == 1))
                m.then_inc(s["kv_done"], 1)
                if not first:
                    pe.wait_ge(s["q_out"], c)
                pe.matmul(q_ps[:, 0:H], ones_bf[0:3, :], bparts[:, BQ], start=True, stop=False)
                for k in range(2):
                    m = pe.matmul(q_ps[:, 0:H], xnT[:, 0, k, :], wqs[:, k, :], start=False, stop=(k == 1))
                m.then_inc(s["q_done"], 1)

            for t in range(NG):
                node_tile(t, 0, t, t == 0)
            with pe.Fori(1, NGROUPS) as g:
                for t in range(NG):
                    node_tile(g * NG + t, g, t, False)

        @block.scalar
        def _(act):
            def root(c, k):
                act.wait_ge(s["ve_done"], c + 1)
                act.activation(sd[:, k, :], ve[:, k, :], ACT.Sqrt).then_inc(s["sd_done"], 1)

            def node_scalar(g):
                q = g % 2
                root(2 * g, 0)
                act.wait_ge(s["small"], 12 * g + 6)
                if g >= 1:
                    act.wait_ge(s["xn_done"], g)
                for t in range(NG):
                    act.activation(hg[:, t, :], xg[:, q, t, :], ACT.Relu, bias=nb[:, 0, t:t + 1], scale=rs[:, 0, t:t + 1]).then_inc(s["h_done"], 1)
                root(2 * g + 1, 1)
                act.wait_ge(s["small"], 12 * g + 12)
                act.wait_ge(s["base_done"], g + 1)
                act.dma_start(base[g * NG * P:(g + 1) * NG * P, :].rearrange("(t p) f -> p t f", p=P), xg[:, q]).then_inc(s["base_stored"], 16)
                for t in range(NG):
                    act.activation(hg[:, t, :], hg[:, t, :], ACT.Identity, bias=nb[:, 1, t:t + 1], scale=rs[:, 1, t:t + 1]).then_inc(s["z_done"], 1)
                if g + 2 < NGROUPS:
                    act.wait_ge(s["base_stored"], 16 * (g + 1))
                    load_x(g + 2)
                for t in range(NG):
                    c = g * NG + t
                    act.wait_ge(s["xnt_ps"], c + 1)
                    if c >= 1:
                        act.wait_ge(s["q_done"], c)
                    act.activation(xnT[:, 0, :, :], t_ps[:], ACT.Copy).then_inc(s["xnt_sb"], 1)
                    act.wait_ge(s["kv_done"], c + 1)
                    act.activation(kvx[:, t, 0:H], kv_ps[:, 0:H], ACT.Copy)
                    act.activation(kvx[:, t, H:2 * H], kv_ps[:, H:2 * H], ACT.Copy, scale=gate_b[:, 0:1]).then_inc(s["kv_out"], 1)
                    act.wait_ge(s["q_done"], c + 1)
                    if t == 0 and g >= 1:
                        act.wait_ge(s["q_lo"], g)
                        act.wait_ge(s["q_stored"], 16 * g)
                    act.activation(qf[:, t, :], q_ps[:, 0:H], ACT.Copy).then_inc(s["q_out"], 1)
                    act.wait_ge(s["q_out"], c + 1)
                    act.activation(q3[:, t, 0, :], qf[:, t, :], ACT.Copy).then_inc(s["q_hi"], 1)
                act.wait_ge(s["kv_out"], (g + 1) * NG)
                act.dma_start(table[g * NG * P:(g + 1) * NG * P, :].rearrange("(t p) f -> p t f", p=P), kvx[:]).then_inc(s["table_stored"], 16)
                act.wait_ge(s["q_lo"], g + 1)
                act.dma_start(qparts[g * NG * P:(g + 1) * NG * P, :].rearrange("(t p) f -> p t f", p=P),
                              q3[:].rearrange("p t k f -> p t (k f)")).then_inc(s["q_stored"], 16)

            def load_x(g):
                q = g % 2
                rows = x[g * NG * P:min((g + 1) * NG * P, N), :]
                if g < NGROUPS - 1:
                    half = NG // 2
                    for a, b in ((0, half), (half, NG)):
                        act.dma_start(xg[:, q, a:b, :], rows[a * P:b * P, :].rearrange("(t p) f -> p t f", p=P)).then_inc(s[f"x_loaded{q}"], 16)
                    return
                act.activation(xg[:, q, NG - 1, :], xg[:, q, NG - 1, :], ACT.Copy, scale=0.0).then_inc(s["stored"], 1)
                act.wait_ge(s["stored"], 1)
                act.dma_start(xg[:, q, 0:NG - 1, :], rows[0:(NG - 1) * P, :].rearrange("(t p) f -> p t f", p=P)).then_inc(s[f"x_loaded{q}"], 16)
                act.dma_start(xg[0:LAST_ROWS, q, NG - 1, :], rows[(NG - 1) * P:, :]).then_inc(s[f"x_loaded{q}"], 16)

            load_x(0)
            load_x(1)
            act.wait_ge(s["params_loaded"], NPAR)
            for g in range(NGROUPS):
                node_scalar(g)
            act.wait_ge(s["base_stored"], 16 * NGROUPS)
            act.wait_ge(s["table_stored"], 16 * NGROUPS)
            act.wait_ge(s["q_stored"], 16 * NGROUPS)


def edges(nc, sb_, sem, recs, table, qparts, ident, ones_bf, iota1, w1s, w2s, bparts, unit_bucket, aggr, B2):
    with ExitStack() as st:
        def sb(name, shape, dt=F32):
            return st.enter_context(nc.sbuf_tensor(name, shape, dt))

        def ps(name, shape, dt=F32):
            return st.enter_context(nc.psum_tensor(name, shape, dt))

        rec = sb("urec", [P, DEPTH, 2, REC])
        dst_i = sb("udst", [P, DEPTH, 2], I32)
        qb = sb("uq", [P, DEPTH, 3, H], BF16)
        kvx = sb("ukvx", [P, DEPTH, 2, TAB])
        oh = sb("uonehot", [P, DEPTH, 2, P])
        ohT = sb("uonehotT", [P, 2, 2, P], BF16)
        rT = sb("urT", [NRBF + 1, 2, 2 * P])
        th = sb("utanh", [P, 2, 2, UNIT])
        hid = sb("uhid", [P, 2, 2, UNIT])
        prod = sb("uprod", [P, 2, 2 * NH, HD])
        sc = sb("uscores", [P, 2, 2, NH])
        mx = sb("umax", [P, 2, 2])
        ex = sb("uexp", [P, 2, 2, NH])
        sm = sb("usum", [P, 2, 2])
        rc = sb("urecip", [P, 2, 2])
        at = sb("uattn", [P, 2, 2, NH])
        av = sb("uav", [P, 2, 2, H])
        phys = sb("uphys", [P, 2, 2, H])
        msg = sb("umsg", [P, 2, 2, H])
        turn_ps = [ps(f"turn_ps{k}", [P, 4, P]) for k in range(2)]
        hid_ps = [ps(f"hid_ps{k}", [P, 2, UNIT]) for k in range(2)]
        q_ps = [ps(f"uq_ps{k}", [P, 2, H]) for k in range(2)]
        w_ps = ps("w_ps", [P, 2, H])
        ag_ps = ps("ag_ps", [P, 512])

        s = {n: sem("u_" + n) for n in (
            "zeroed", "dst_ready", "dst_waited", "onehot_ready", "turned", "rT_ready", "hid_done", "qe_done", "tanh_ready",
            "hid_ready", "w_done", "qk_done", "scored", "weighted", "max_done", "shifted", "exp_ready", "sum_done",
            "recip_done", "attn_ready", "av_done", "phys_done", "msg_ready", "ag_done", "ag_added")}
        rec_in = [sem(f"u_rec_in{k}") for k in range(DEPTH)]
        q_in = [sem(f"u_q_in{k}") for k in range(DEPTH)]
        kvx_in = [sem(f"u_kvx_in{k}") for k in range(DEPTH)]
        TURNS = UNITS // DEPTH
        rec_v = recs.rearrange("(u p j) f -> u p j f", p=P, j=2)
        q_v = qparts.rearrange("(b p) f -> b p f", p=P)

        def turns(eng, body):
            for k in range(DEPTH):
                body(k, k, 0, True)
            with eng.Fori(1, TURNS) as i:
                for k in range(DEPTH):
                    body(i * DEPTH + k, k, i, False)

        block = st.enter_context(nc.Block())

        @block.sync
        def _(sp):
            def unit(u, k, i, first):
                if not first:
                    sp.wait_ge(s["msg_ready"], u - (DEPTH - 1))
                sp.dma_start(rec[:, k], rec_v[u] if first else rec_v[bass.ds(u, 1)].rearrange("a p j f -> p (a j) f")).then_inc(rec_in[k], 16)
                b = sp.value_load(unit_bucket[0:1, u:u + 1] if first else unit_bucket[0:1, bass.ds(u, 1)], min_val=0, max_val=BUCKETS - 1)
                sp.dma_start(qb[:, k], q_v[bass.ds(b, 1)].rearrange("a p (k f) -> p (a k) f", k=3)).then_inc(q_in[k], 16)
            turns(sp, unit)

        @block.gpsimd
        def _(pool):
            def unit(u, k, i, first):
                pool.wait_ge(s["dst_ready"], u + 1)
                pool.sem_inc(s["dst_waited"], 1)
                for j in range(2):
                    pool.indirect_dma_start(kvx[:, k, j, :], None, table,
                                            bass.IndirectOffsetOnAxis(ap=dst_i[:, k, j:j + 1], axis=0)).then_inc(kvx_in[k], 16)
            turns(pool, unit)

        @block.scalar
        def _(act):
            def destinations(u, k, i):
                act.wait_ge(rec_in[k], i * 16 + 16)
                act.activation(dst_i[:, k, :], rec[:, k, :, R_DST], ACT.Copy).then_inc(s["dst_ready"], 1)

            def evacuate(u, k, i, first):
                q = k % 2
                act.wait_ge(s["turned"], u + 1)
                if not (first and k < 2):
                    act.wait_ge(s["qe_done"], u - 1)
                act.activation(rT[:, q, :].rearrange("p (j e) -> p j e", j=2), turn_ps[q][0:NRBF + 1, 0:2, :], ACT.Copy)
                act.activation(ohT[:, q], turn_ps[q][:, 2:4, :], ACT.Copy).then_inc(s["rT_ready"], 1)

            def tanh(u, k, i, first):
                q = k % 2
                act.wait_ge(s["hid_done"], u + 1)
                if not (first and k < 2):
                    act.wait_ge(s["hid_ready"], u - 1)
                act.activation(th[:, q], hid_ps[q][:], ACT.Tanh, scale=0.5).then_inc(s["tanh_ready"], 1)

            def exponent(u, k, i, first):
                q = k % 2
                act.wait_ge(s["shifted"], u + 1)
                act.activation(ex[:, q], sc[:, q], ACT.Exp, scale=float(HD) ** -0.5).then_inc(s["exp_ready"], 1)

            AHEAD = 2
            for k in range(AHEAD):
                destinations(k, k, 0)

            def unit(u, k, i, first):
                evacuate(u, k, i, first)
                k2 = (k + AHEAD) % DEPTH
                i2 = i + (k + AHEAD) // DEPTH
                if last_turn:
                    if k + AHEAD < DEPTH:
                        destinations(u + AHEAD, k2, i2)
                else:
                    destinations(u + AHEAD, k2, i2)
                tanh(u, k, i, first)
                exponent(u, k, i, first)

            last_turn = False
            for k in range(DEPTH):
                unit(k, k, 0, True)
            with act.Fori(1, TURNS - 1) as i:
                for k in range(DEPTH):
                    unit(i * DEPTH + k, k, i, False)
            last_turn = True
            for k in range(DEPTH):
                unit((TURNS - 1) * DEPTH + k, k, TURNS - 1, False)

        @block.tensor
        def _(pe):
            def turn(u, k, i, first):
                q = k % 2
                pe.wait_ge(rec_in[k], i * 16 + 16)
                pe.wait_ge(s["onehot_ready"], u + 1)
                if not (first and k < 2):
                    pe.wait_ge(s["rT_ready"], u - 1)
                for j in range(2):
                    pe.transpose(turn_ps[q][0:NRBF + 1, j, :], rec[:, k, j, 0:NRBF + 1], ident[:])
                for j in range(2):
                    m = pe.transpose(turn_ps[q][:, 2 + j, :], oh[:, k, j, :], ident[:])
                m.then_inc(s["turned"], 1)

            def hidden_and_q(u, k, i, first):
                q = k % 2
                pe.wait_ge(s["rT_ready"], u + 1)
                if not (first and k < 2):
                    pe.wait_ge(s["hid_ready"], u - 1)
                for c in range(2):
                    m = pe.matmul(hid_ps[q][:, c, :], w1s[:, c * P:(c + 1) * P], rT[:, q, :], start=(c == 0), stop=True, skip_group_check=True)
                m.then_inc(s["hid_done"], 1)
                pe.wait_ge(q_in[k], i * 16 + 16)
                if not (first and k < 2):
                    pe.wait_ge(s["qk_done"], u - 1)
                for j in range(2):
                    for part in range(3):
                        m = pe.matmul(q_ps[q][:, j, :], ohT[:, q, j, :], qb[:, k, part, :], start=(j == 0 and part == 0), stop=(part == 2), skip_group_check=True)
                m.then_inc(s["qe_done"], 1)

            def filters(u, k, i, first):
                q = k % 2
                pe.wait_ge(s["hid_ready"], u + 1)
                if not (first and k < 1):
                    pe.wait_ge(s["phys_done"], u)
                for j in range(2):
                    pe.matmul(w_ps[:, j, :], ones_bf[0:3, :], bparts[:, B2], start=(j == 0), stop=False, skip_group_check=True)
                    for c in range(2):
                        m = pe.matmul(w_ps[:, j, :], hid[:, q, c, j * P:(j + 1) * P], w2s[:, c, :], start=False, stop=(c == 1), skip_group_check=True)
                m.then_inc(s["w_done"], 1)

            def aggregate(u, k, i, first):
                q = k % 2
                pe.wait_ge(s["msg_ready"], u + 1)
                if not (first and k < 1):
                    pe.wait_ge(s["ag_added"], u)
                for j in range(2):
                    m = pe.matmul(ag_ps[:, 0:H], oh[:, k, j, :], msg[:, q, j, :], start=(j == 0), stop=(j == 1))
                m.then_inc(s["ag_done"], 1)

            def unit(u, k, i, first):
                turn(u, k, i, first)
                if not (first and k < 1):
                    filters(u - 1, (k - 1) % DEPTH, i - (k < 1), first)
                hidden_and_q(u, k, i, first)
                if not (first and k < 2):
                    aggregate(u - 2, (k - 2) % DEPTH, i - (k < 2), first)
            turns(pe, unit)
            U = UNITS
            filters(U - 1, DEPTH - 1, TURNS - 1, False)
            aggregate(U - 2, DEPTH - 2, TURNS - 1, False)
            aggregate(U - 1, DEPTH - 1, TURNS - 1, False)

        @block.vector
        def _(dve):
            dve.memset(aggr[:], 0.0).then_inc(s["zeroed"], 1)

            def select(u, k, i, first):
                dve.wait_ge(rec_in[k], i * 16 + 16)
                dve.tensor_tensor(oh[:, k], rec[:, k, :, R_LOC:R_LOC + 1].to_broadcast([P, 2, P]),
                                  iota1[:].unsqueeze(1).to_broadcast([P, 2, P]), ALU.is_equal).then_inc(s["onehot_ready"], 1)

            def message(u, k, i, first):
                q = k % 2
                dve.wait_ge(s["w_done"], u + 1)
                for j in range(2):
                    m = dve.scalar_tensor_tensor(phys[:, q, j, :], w_ps[:, j, :], rec[:, k, j, R_W:R_W + 1], kvx[:, k, j, 2 * H:3 * H], ALU.mult, ALU.mult)
                m.then_inc(s["phys_done"], 1)
                dve.wait_ge(s["phys_done"], u + 1)
                dve.wait_ge(s["av_done"], u + 1)
                dve.tensor_tensor(msg[:, q], phys[:, q], av[:, q], ALU.add).then_inc(s["msg_ready"], 1)

            def silu(u, k, i, first):
                q = k % 2
                dve.wait_ge(s["tanh_ready"], u + 1)
                if not (first and k < 2):
                    dve.wait_ge(s["w_done"], u - 1)
                dve.scalar_tensor_tensor(hid[:, q], th[:, q], 1.0, hid_ps[q][:], ALU.add, ALU.mult).then_inc(s["hid_ready"], 1)

            def scores(u, k, i, first):
                q = k % 2
                dve.wait_ge(s["qe_done"], u + 1)
                dve.wait_ge(kvx_in[k], i * 32 + 32)
                dve.tensor_tensor(prod[:, q].rearrange("p (j h) d -> p j (h d)", j=2), q_ps[q][:], kvx[:, k, :, 0:H], ALU.mult).then_inc(s["qk_done"], 1)
                dve.wait_ge(s["qk_done"], u + 1)
                dve.tensor_reduce(sc[:, q].rearrange("p j h -> p (j h)"), prod[:, q], AX_X, ALU.add).then_inc(s["scored"], 1)
                dve.wait_ge(s["scored"], u + 1)
                dve.tensor_tensor(sc[:, q], sc[:, q], rec[:, k, :, R_W:R_W + 1].to_broadcast([P, 2, NH]), ALU.mult).then_inc(s["weighted"], 1)
                dve.wait_ge(s["weighted"], u + 1)
                dve.tensor_reduce(mx[:, q], sc[:, q], AX_X, ALU.max).then_inc(s["max_done"], 1)
                dve.wait_ge(s["max_done"], u + 1)
                dve.tensor_tensor(sc[:, q], sc[:, q], mx[:, q].unsqueeze(2).to_broadcast([P, 2, NH]), ALU.subtract).then_inc(s["shifted"], 1)

            def attend(u, k, i, first):
                q = k % 2
                dve.wait_ge(s["exp_ready"], u + 1)
                dve.tensor_reduce(sm[:, q], ex[:, q], AX_X, ALU.add).then_inc(s["sum_done"], 1)
                dve.wait_ge(s["sum_done"], u + 1)
                dve.reciprocal(rc[:, q], sm[:, q]).then_inc(s["recip_done"], 1)
                dve.wait_ge(s["recip_done"], u + 1)
                dve.tensor_tensor(at[:, q], ex[:, q], rc[:, q].unsqueeze(2).to_broadcast([P, 2, NH]), ALU.mult).then_inc(s["attn_ready"], 1)
                dve.wait_ge(s["attn_ready"], u + 1)
                for j in range(2):
                    m = dve.tensor_tensor(av[:, q, j, :].rearrange("p (h d) -> p h d", h=NH), kvx[:, k, j, H:2 * H].rearrange("p (h d) -> p h d", h=NH),
                                          at[:, q, j, :].unsqueeze(2).to_broadcast([P, NH, HD]), ALU.mult)
                m.then_inc(s["av_done"], 1)

            def add_up(u, k, i, first):
                b = dve.value_load(unit_bucket[0:1, u:u + 1] if isinstance(u, int) else unit_bucket[0:1, bass.ds(u, 1)], min_val=0, max_val=BUCKETS - 1)
                dve.wait_ge(s["ag_done"], u + 1)
                if not (first and k < 1):
                    dve.wait_ge(s["ag_added"], u)
                row = aggr[:, bass.ds(b, 1), :].rearrange("p a f -> p (a f)")
                dve.tensor_tensor(row, row, ag_ps[:, 0:H], ALU.add).then_inc(s["ag_added"], 1)

            select(0, 0, 0, True)
            dve.wait_ge(s["zeroed"], 1)

            def unit(u, k, i, first):
                if not (first and k < 1):
                    message(u - 1, (k - 1) % DEPTH, i - (k < 1), first)
                k1 = (k + 1) % DEPTH
                if not (last_turn and k == DEPTH - 1):
                    select(u + 1, k1, i + (k + 1) // DEPTH, first)
                silu(u, k, i, first)
                scores(u, k, i, first)
                if not (first and k < 2):
                    add_up(u - 2, (k - 2) % DEPTH, i - (k < 2), first and k == 2)
                attend(u, k, i, first)

            last_turn = False
            for k in range(DEPTH):
                unit(k, k, 0, True)
            with dve.Fori(1, TURNS - 1) as i:
                for k in range(DEPTH):
                    unit(i * DEPTH + k, k, i, False)
            last_turn = True
            for k in range(DEPTH):
                unit((TURNS - 1) * DEPTH + k, k, TURNS - 1, False)
            U = UNITS
            message(U - 1, DEPTH - 1, TURNS - 1, False)
            add_up(U - 2, DEPTH - 2, TURNS - 1, False)
            add_up(U - 1, DEPTH - 1, TURNS - 1, False)


def finish(nc, sb_, sem, base, out, ident, ones_bf, wos, bparts, aggr, BO):
    with ExitStack() as st:
        def sb(name, shape, dt=F32):
            return st.enter_context(nc.sbuf_tensor(name, shape, dt))

        def ps(name, shape, dt=F32):
            return st.enter_context(nc.psum_tensor(name, shape, dt))

        ag = sb("fag", [P, 2, H])
        agT = sb("fagT", [P, 2, 2, P])
        bs = sb("fbase", [P, 2, H])
        ot = sb("fout", [P, 2, H])
        t_ps = [ps(f"ft_ps{k}", [P, 4, P]) for k in range(2)]
        o_ps = [ps(f"fo_ps{k}", [P, 512]) for k in range(2)]
        s = {n: sem("f_" + n) for n in ("copied", "turned", "turned_out", "projected", "summed")}
        base_in = [sem(f"f_base_in{k}") for k in range(2)]
        stored = [sem(f"f_stored{k}") for k in range(2)]
        base_v = base.rearrange("(b p) f -> b p f", p=P)
        out_v = out[0:(BUCKETS - 1) * P, :].rearrange("(b p) f -> b p f", p=P)
        HALF = BUCKETS // 2
        block = st.enter_context(nc.Block())

        @block.sync
        def _(sp):
            for q in range(2):
                sp.dma_start(bs[:, q], base_v[q]).then_inc(base_in[q], 16)
            with sp.Fori(1, HALF) as i:
                for q in range(2):
                    sp.wait_ge(s["summed"], i * 2 + q - 1)
                    sp.dma_start(bs[:, q], base_v[bass.ds(i * 2 + q, 1)].rearrange("a p f -> p (a f)")).then_inc(base_in[q], 16)

        @block.gpsimd
        def _(pool):
            def store(b, q):
                pool.wait_ge(s["summed"], b + 1)
                pool.dma_start(out_v[bass.ds(b, 1)].rearrange("a p f -> p (a f)"), ot[:, q]).then_inc(stored[q], 16)
            with pool.Fori(0, HALF - 1) as i:
                for q in range(2):
                    store(i * 2 + q, q)
            pool.wait_ge(s["summed"], BUCKETS - 1)
            pool.dma_start(out_v[BUCKETS - 2], ot[:, 0]).then_inc(stored[0], 16)
            pool.wait_ge(s["summed"], BUCKETS)
            pool.dma_start(out[(BUCKETS - 1) * P:N, :], ot[0:LAST_ROWS, 1]).then_inc(stored[1], 16)
            for q in range(2):
                pool.wait_ge(stored[q], 16 * HALF)

        @block.scalar
        def _(act):
            def tile(b, q, first):
                act.wait_ge(s["turned"], b + 1)
                if not first:
                    act.wait_ge(s["projected"], b - 1)
                act.activation(agT[:, q], t_ps[q][:, 0:2, :], ACT.Copy).then_inc(s["turned_out"], 1)
            for q in range(2):
                tile(q, q, True)
            with act.Fori(1, HALF) as i:
                for q in range(2):
                    tile(i * 2 + q, q, False)

        @block.tensor
        def _(pe):
            def tile(b, q, first):
                pe.wait_ge(s["copied"], b + 1)
                if not first:
                    pe.wait_ge(s["turned_out"], b - 1)
                for c in range(2):
                    m = pe.transpose(t_ps[q][:, c, :], ag[:, q, c * P:(c + 1) * P], ident[:])
                m.then_inc(s["turned"], 1)
                pe.wait_ge(s["turned_out"], b + 1)
                if not first:
                    pe.wait_ge(s["summed"], b - 1)
                pe.matmul(o_ps[q][:, 0:H], ones_bf[0:3, :], bparts[:, BO], start=True, stop=False)
                for c in range(2):
                    m = pe.matmul(o_ps[q][:, 0:H], agT[:, q, c, :], wos[:, c, :], start=False, stop=(c == 1))
                m.then_inc(s["projected"], 1)
            for q in range(2):
                tile(q, q, True)
            with pe.Fori(1, HALF) as i:
                for q in range(2):
                    tile(i * 2 + q, q, False)

        @block.vector
        def _(dve):
            def copy(b, q, first):
                if not first:
                    dve.wait_ge(s["turned"], b - 1)
                dve.tensor_copy(ag[:, q], aggr[:, b, :] if first else aggr[:, bass.ds(b, 1), :].rearrange("p a f -> p (a f)")).then_inc(s["copied"], 1)

            def total(b, q, i, first):
                dve.wait_ge(s["projected"], b + 1)
                dve.wait_ge(base_in[q], i * 16 + 16)
                if not first:
                    dve.wait_ge(stored[q], i * 16)
                dve.tensor_tensor(ot[:, q], o_ps[q][:, 0:H], bs[:, q], ALU.add).then_inc(s["summed"], 1)
            for q in range(2):
                copy(q, q, True)
            for q in range(2):
                total(q, q, 0, True)
            with dve.Fori(1, HALF) as i:
                for q in range(2):
                    copy(i * 2 + q, q, False)
                for q in range(2):
                    total(i * 2 + q, q, i, False)


_INS = ["x", "src", "dst", "edge_attr_64", "edge_weight", "L0_gnn_w1", "L0_gnn_b1", "L0_gnn_w2", "L0_gnn_b2", "L0_gnn_ln_w",
        "L0_gnn_ln_b", "L0_gnn_wq", "L0_gnn_bq", "L0_gnn_wk", "L0_gnn_bk", "L0_gnn_wv", "L0_gnn_bv", "L0_gnn_wo", "L0_gnn_bo",
        "L0_gnn_gate"]


def kernel(**inputs):
    import numpy as _np
    import concourse.bacc as _bacc
    from concourse import mybir as _mybir
    from concourse.bass_utils import run_bass_kernel_spmd as _run

    nc = _bacc.Bacc("TRN2", target_bir_lowering=False, num_devices=1)
    arrays, args = {}, []
    for name in _INS:
        a = _np.ascontiguousarray(inputs[name])
        arrays[f"in_{name}"] = a
        args.append(nc.dram_tensor(f"in_{name}", a.shape, _mybir.dt.from_np(a.dtype), kind="ExternalInput").ap())
    args.append(nc.dram_tensor("out", (N, H), F32, kind="ExternalOutput").ap())
    build(nc, *args)
    r = _run(nc, [arrays], core_ids=[0])
    return r.results[0]["out"]
```

```python
from contextlib import ExitStack

import concourse.bass as bass
from concourse import mybir

F32 = mybir.dt.float32
BF16 = mybir.dt.bfloat16
I32 = mybir.dt.int32
ALU = mybir.AluOpType
ACT = mybir.ActivationFunctionType
AX_X = mybir.AxisListType.X

P = 128
N = 12500
E = 212500
H = 256
NH, HD = 8, 32
NRBF = 64
EPS = 1e-5
BUCKETS = -(-N // P)
NPAD = BUCKETS * P
LAST_ROWS = N - (BUCKETS - 1) * P
COLS = E // P
TAIL = E - COLS * P
RCOLS = 4
RGROUPS = -(-(COLS + 1) // RCOLS)
CPAD = RGROUPS * RCOLS
NOBUCKET = 200
SCOLS = 10
SGROUPS = COLS // SCOLS
SHIFT = 7
UNIT = 2 * P
USHIFT = 8
OHDEPTH = 8
LAG = 3
DEPTH = 8
KVDEPTH = 4
UNITS = -(-((E + BUCKETS * (UNIT - 1)) // UNIT) // DEPTH) * DEPTH
SLOTS = UNITS * UNIT
REC = NRBF + 4
R_ONE, R_W, R_DST, R_LOC = NRBF, NRBF + 1, NRBF + 2, NRBF + 3
TAB = 3 * H
NG = 7
NGROUPS = BUCKETS // NG
ZROWS = 16
ZPER = SLOTS // P


def build(nc, x, src, dst, rbf, weight, w1, b1, w2, b2, ln_w, ln_b, wq, bq, wk, bk, wv, bv, wo, bo, gate, out):
    recs = nc.dram_tensor("records", [SLOTS, REC], F32).ap()
    table = nc.dram_tensor("kvx_table", [NPAD, TAB], F32).ap()
    qparts = nc.dram_tensor("q_parts", [NPAD, 3 * H], BF16).ap()
    base = nc.dram_tensor("x_plus_h", [NPAD, H], F32).ap()
    with ExitStack() as ctx:
        def sb(name, shape, dt, stack=ctx):
            return stack.enter_context(nc.sbuf_tensor(name, shape, dt))

        def sem(name):
            return ctx.enter_context(nc.semaphore(name))

        ident = sb("ident", [P, P], F32)
        ones_bf = sb("ones_bf", [P, P], BF16)
        iota1 = sb("iota1", [P, P], F32)
        w1s = sb("w1s", [NRBF + 1, H], F32)
        w2s = sb("w2s", [P, 2, H], F32)
        wos = sb("wos", [P, 2, H], F32)
        bparts = sb("bparts", [3, 6 * H], BF16)
        unit_bucket = sb("unit_bucket", [1, UNITS], I32)
        lagged_bucket = sb("lagged_bucket", [1, UNITS + DEPTH], I32)
        BQ, BK, BV, B2, BO = (slice(k * H, (k + 1) * H) for k in (0, 1, 2, 3, 4))
        BKV = slice(H, 3 * H)

        prep(nc, ctx, sb, sem, x, src, dst, rbf, weight, w1, b1, w2, b2, ln_w, ln_b, wq, bq, wk, bk, wv, bv, wo, bo,
             gate, recs, table, qparts, base, ident, ones_bf, iota1, w1s, w2s, wos, bparts, unit_bucket, lagged_bucket, BQ, BKV)
        aggr = sb("aggr", [P, BUCKETS, H], F32)
        edges(nc, sb, sem, recs, table, qparts, ident, ones_bf, iota1, w1s, w2s, bparts, unit_bucket, lagged_bucket, aggr, B2)
        finish(nc, sb, sem, base, out, ident, ones_bf, wos, bparts, aggr, BO)


def prep(nc, ctx, sb_, sem, x, src, dst, rbf, weight, w1, b1, w2, b2, ln_w, ln_b, wq, bq, wk, bk, wv, bv, wo, bo,
         gate, recs, table, qparts, base, ident, ones_bf, iota1, w1s, w2s, wos, bparts, unit_bucket, lagged_bucket, BQ, BKV):
    with ExitStack() as st:
        def sb(name, shape, dt):
            return st.enter_context(nc.sbuf_tensor(name, shape, dt))

        def ps(name, shape, dt=F32):
            return st.enter_context(nc.psum_tensor(name, shape, dt))

        src_i = sb("src_i", [P, CPAD], I32)
        dst_i = sb("dst_i", [P, CPAD], I32)
        tmp_i = sb("tmp_i", [P, CPAD], I32)
        wgt = sb("wgt", [P, CPAD], F32)
        bucket = sb("bucket", [P, CPAD], BF16)
        meta = sb("meta", [P, CPAD, 4], F32)
        pos = sb("pos", [P, CPAD], F32)
        eq = sb("eq", [P, 2, CPAD], BF16)
        bucket_ids = sb("bucket_ids", [P, BUCKETS], F32)
        bucket_ids_bf = sb("bucket_ids_bf", [P, BUCKETS], BF16)
        tri = sb("tri", [P, P], BF16)
        ones_f = sb("ones_f", [P, P], F32)
        count = sb("count", [P, BUCKETS], F32)
        zero98 = sb("zero98", [P, BUCKETS], F32)
        units_i = sb("units_i", [P, BUCKETS], I32)
        units_f = sb("units_f", [P, BUCKETS], F32)
        end_f = sb("end_f", [P, BUCKETS], F32)
        end_col = sb("end_col", [BUCKETS, 1], F32)
        unit_no = sb("unit_no", [BUCKETS, UNITS], F32)
        carry = sb("carry", [P, 2, BUCKETS], F32)
        onehot = sb("onehot", [P, 2, RCOLS, BUCKETS], BF16)
        ranked = sb("ranked", [P, 2, RCOLS, BUCKETS], F32)
        rec = sb("rec", [P, 2, SCOLS, REC], F32)
        slot_i = sb("slot_i", [P, 2, SCOLS], I32)
        tail_rec = sb("tail_rec", [P, REC], F32)
        tail_slot = sb("tail_slot", [P, 1], I32)
        zero = sb("zero", [P, ZROWS * REC], F32)
        bias_f = sb("bias_f", [3, 6 * H], F32)
        bias_r = sb("bias_r", [3, 6 * H], F32)
        bias_p = sb("bias_p", [3, 3, 6 * H], BF16)
        w2raw = sb("w2raw", [P, 2, H], F32)
        wqs = sb("wqs", [P, 2, H], F32)
        wkvs = sb("wkvs", [P, 2, 2 * H], F32)
        lnw_b = sb("lnw_b", [P, H], F32)
        lnb_b = sb("lnb_b", [P, H], F32)
        gate_b = sb("gate_b", [P, 1], F32)
        xg = sb("xg", [P, 2, NG, H], F32)
        hg = sb("hg", [P, NG, H], F32)
        stats = sb("stats", [P, NG, 6], F32)
        mv = sb("mv", [P, 2, NG, 2], F32)
        ve = sb("ve", [P, 2, NG], F32)
        sd = sb("sd", [P, 2, NG], F32)
        rs = sb("rs", [P, 2, NG], F32)
        r2 = sb("r2", [P, 2, NG], F32)
        nb = sb("nb", [P, 2, NG], F32)
        kvx = sb("kvx", [P, NG, TAB], F32)
        qf = sb("qf", [P, NG, H], F32)
        qr = sb("qr", [P, NG, H], F32)
        q3 = sb("q3", [P, NG, 3, H], BF16)
        xnT = sb("xnT", [P, 2, 2, P], F32)

        rank_ps = ps("rank_ps", [P, 2, 512])
        setup_ps = ps("setup_ps", [P, 2, 512])
        t_ps = ps("t_ps", [P, 2, P])
        t_ps_pad = ps("t_ps_pad", [P, 256])
        kv_ps = ps("kv_ps", [P, 512])
        q_ps = ps("q_ps", [P, 512])

        s = {n: sem("a_" + n) for n in (
            "edges_loaded", "params_loaded", "filled", "consts", "v", "pe_setup", "dve_setup", "onehot_ready",
            "carry_ready", "ranks_ready", "ranks_picked", "positions_ready", "stored", "zeros_stored", "stats_waited", "placed_waited",
            "placed", "loaded_tail", "tail_stored",
            "x_loaded0", "x_loaded1", "stats_done", "aggregated", "ve_done", "sd_done", "small", "bias_done",
            "h_done", "base_done", "base_stored", "z_done", "lnw_done", "xn_done", "xnt_ps", "xnt_sb", "kv_done", "q_done", "kv_out", "q_out",
            "q_hi", "q_rest", "q_mid", "q_lo", "table_stored", "q_stored")}
        rec_loaded = [sem(f"a_rec_loaded{q}") for q in range(2)]
        scattered = [sem(f"a_scattered{q}") for q in range(2)]

        rbf_v = rbf[0:COLS * P, :].rearrange("(p t) f -> p t f", p=P)
        rec_v = recs.rearrange("(p s) f -> p (s f)", p=P)
        NEDGE = 16 * 6
        NPAR = 16 * 16

        block = st.enter_context(nc.Block())

        @block.sync
        def _(sp):
            sp.wait_ge(s["filled"], 3)
            for to, of in ((src_i, src), (dst_i, dst), (wgt, weight)):
                sp.dma_start(to[:, 0:COLS], of[0:COLS * P].rearrange("(p t) -> p t", p=P)).then_inc(s["edges_loaded"], 16)
                sp.dma_start(to[0:TAIL, COLS:COLS + 1], of[COLS * P:E].rearrange("(p t) -> p t", t=1)).then_inc(s["edges_loaded"], 16)
            for to, of in ((w1s[0:NRBF, :], w1), (w1s[NRBF:NRBF + 1, :], b1.rearrange("(a n) -> a n", a=1)),
                           (w2raw[:], w2.rearrange("(c p) n -> p c n", p=P)), (wos[:], wo.rearrange("(c p) n -> p c n", p=P)),
                           (wqs[:], wq.rearrange("(c p) n -> p c n", p=P)),
                           (wkvs[:, :, 0:H], wk.rearrange("(c p) n -> p c n", p=P)),
                           (wkvs[:, :, H:2 * H], wv.rearrange("(c p) n -> p c n", p=P)),
                           (lnw_b[:], ln_w.partition_broadcast(P)), (lnb_b[:], ln_b.partition_broadcast(P)),
                           (gate_b[:], gate.partition_broadcast(P)),
                           (bias_f[:, 0:H], bq.partition_broadcast(3)), (bias_f[:, H:2 * H], bk.partition_broadcast(3)),
                           (bias_f[:, 2 * H:3 * H], bv.partition_broadcast(3)), (bias_f[:, 3 * H:4 * H], b2.partition_broadcast(3)),
                           (bias_f[:, 4 * H:5 * H], bo.partition_broadcast(3)), (bias_f[:, 5 * H:6 * H], bo.partition_broadcast(3))):
                sp.dma_start(to, of).then_inc(s["params_loaded"], 16)
            sp.wait_ge(s["consts"], 1)
            for k in range(0, ZPER, 8 * ZROWS):
                n = min(8 * ZROWS, ZPER - k) // ZROWS
                sp.dma_start(rec_v[:, k * REC:(k + n * ZROWS) * REC].rearrange("p (n f) -> p n f", n=n),
                             zero[:, :].unsqueeze(1).to_broadcast([P, n, ZROWS * REC])).then_inc(s["zeros_stored"], 16)
            sp.dma_start(tail_rec[0:TAIL, 0:NRBF], rbf[COLS * P:E, :]).then_inc(s["loaded_tail"], 16)
            for q in range(2):
                sp.dma_start(rec[:, q, :, 0:NRBF], rbf_v[:, q * SCOLS:(q + 1) * SCOLS, :]).then_inc(rec_loaded[q], 16)
            with sp.Fori(1, SGROUPS // 2) as i:
                for q in range(2):
                    sp.wait_ge(scattered[q], i * (16 * SCOLS))
                    sp.dma_start(rec[:, q, :, 0:NRBF], rbf_v[:, bass.ds((2 * i + q) * SCOLS, SCOLS), :]).then_inc(rec_loaded[q], 16)

        @block.gpsimd
        def _(pool):
            pool.memset(src_i[:, COLS:CPAD], NOBUCKET << SHIFT).then_inc(s["filled"], 1)
            pool.memset(dst_i[:, COLS:CPAD], 0).then_inc(s["filled"], 1)
            pool.memset(wgt[:, COLS:CPAD], 0.0).then_inc(s["filled"], 1)
            pool.memset(zero[:, :], 0.0).then_inc(s["consts"], 1)
            pool.memset(ident[:, :], 0.0).then_inc(s["consts"], 1)
            pool.memset(ones_bf[:, :], 1.0).then_inc(s["consts"], 1)
            pool.memset(ones_f[:, :], 1.0).then_inc(s["consts"], 1)
            pool.memset(zero98[:, :], 0.0).then_inc(s["consts"], 1)
            pool.iota(iota1[:, :], [[1, P]], base=1, channel_multiplier=0, allow_small_or_imprecise_dtypes=True).then_inc(s["consts"], 1)
            pool.iota(bucket_ids[:, :], [[1, BUCKETS]], base=0, channel_multiplier=0, allow_small_or_imprecise_dtypes=True).then_inc(s["consts"], 1)
            pool.iota(unit_no[:, :], [[1, UNITS]], base=0, channel_multiplier=0, allow_small_or_imprecise_dtypes=True).then_inc(s["consts"], 1)
            pool.wait_ge(s["consts"], 8)
            pool.affine_select(out=ident[:, :], in_=ident[:, :], compare_op=ALU.not_equal, fill=1.0, base=0,
                               pattern=[[-1, P]], channel_multiplier=1).then_inc(s["consts"], 1)
            pool.affine_select(out=tri[:, :], in_=ones_bf[:, :], compare_op=ALU.is_gt, fill=0.0, base=0,
                               pattern=[[1, P]], channel_multiplier=-1).then_inc(s["consts"], 1)
            pool.wait_ge(s["zeros_stored"], 16 * -(-ZPER // (8 * ZROWS)))
            with pool.Fori(0, SGROUPS // 2) as i:
                for q in range(2):
                    pool.wait_ge(rec_loaded[q], i * 16 + 16)
                    pool.wait_ge(s["positions_ready"], i * (2 * SCOLS // RCOLS) + -(-(q + 1) * SCOLS // RCOLS))
                    pool.tensor_copy(rec[:, q, :, NRBF:REC], meta[:, bass.ds((2 * i + q) * SCOLS, SCOLS), :]).then_inc(s["placed"], 1)
                    pool.tensor_copy(slot_i[:, q, :], pos[:, bass.ds((2 * i + q) * SCOLS, SCOLS)]).then_inc(s["placed"], 1)
                    pool.wait_ge(s["placed"], i * 4 + 2 * q + 2)
                    pool.sem_inc(s["placed_waited"], 1)
                    for t in range(SCOLS):
                        pool.indirect_dma_start(recs, bass.IndirectOffsetOnAxis(ap=slot_i[:, q, t:t + 1], axis=0),
                                                rec[:, q, t, :], None).then_inc(scattered[q], 16)
            pool.wait_ge(s["positions_ready"], RGROUPS)
            pool.wait_ge(s["loaded_tail"], 16)
            pool.tensor_copy(tail_rec[0:TAIL, NRBF:REC], meta[0:TAIL, COLS, :]).then_inc(s["placed"], 1)
            pool.tensor_copy(tail_slot[0:TAIL, :], pos[0:TAIL, COLS:COLS + 1]).then_inc(s["placed"], 1)
            pool.wait_ge(s["placed"], 2 * SGROUPS + 2)
            pool.indirect_dma_start(recs, bass.IndirectOffsetOnAxis(ap=tail_slot[0:TAIL, :], axis=0),
                                    tail_rec[0:TAIL, :], None).then_inc(s["tail_stored"], 16)
            pool.wait_ge(s["tail_stored"], 16)
            for q in range(2):
                pool.wait_ge(scattered[q], 16 * SCOLS * SGROUPS // 2)

        @block.vector
        def _(dve):
            steps = [0]

            def link(ins):
                steps[0] += 1
                ins.then_inc(s["v"], 1)
                dve.wait_ge(s["v"], steps[0])

            dve.wait_ge(s["edges_loaded"], NEDGE)
            dve.wait_ge(s["consts"], 10)
            dve.tensor_copy(bucket_ids_bf[:], bucket_ids[:])
            dve.tensor_copy(meta[:, :, 1], wgt[:])
            dve.tensor_copy(meta[:, :, 2], dst_i[:])
            dve.memset(meta[:, :, 0], 1.0)
            link(dve.tensor_scalar(tmp_i[:], src_i[:], SHIFT, None, ALU.logical_shift_right))
            link(dve.tensor_copy(bucket[:], tmp_i[:]))
            link(dve.tensor_scalar(tmp_i[:], src_i[:], P - 1, None, ALU.bitwise_and))
            link(dve.tensor_scalar(meta[:, :, 3], tmp_i[:], -1.0, -1.0, ALU.mult, ALU.add))
            def tally(b, q):
                dve.tensor_scalar(eq[:, q, :], bucket[:], bucket_ids[:, bass.ds(b, 1)], 0.0, ALU.is_equal, ALU.add,
                                  accum_out=count[:, bass.ds(b, 1)]).then_inc(s["dve_setup"], 1)
            tally(0, 0)
            tally(1, 1)
            with dve.Fori(1, BUCKETS // 2) as i:
                for q in range(2):
                    dve.wait_ge(s["dve_setup"], i * 2 + q - 1)
                    tally(i * 2 + q, q)
            dve.wait_ge(s["pe_setup"], 1)
            link(dve.tensor_scalar(units_i[:], setup_ps[:, 0, 0:BUCKETS], float(UNIT - 1), None, ALU.add))
            link(dve.tensor_scalar(units_i[:], units_i[:], USHIFT, None, ALU.logical_shift_right))
            link(dve.tensor_copy(units_f[:], units_i[:]))
            link(dve.tensor_tensor_scan(end_f[:], units_f[:], zero98[:], 0.0, ALU.add, ALU.add))
            link(dve.tensor_tensor(units_f[:], end_f[:], units_f[:], ALU.subtract))
            dve.tensor_scalar(carry[:, 0, :], units_f[:], float(UNIT), None, ALU.mult).then_inc(s["carry_ready"], 1)

            def make_onehot(g, q):
                dve.tensor_tensor(onehot[:, q, :, :], bucket[:, bass.ds(g * RCOLS, RCOLS)].unsqueeze(2).to_broadcast([P, RCOLS, BUCKETS]),
                                  bucket_ids_bf[:].unsqueeze(1).to_broadcast([P, RCOLS, BUCKETS]), ALU.is_equal).then_inc(s["onehot_ready"], 1)

            def pick_ranks(g, q):
                r = rank_ps[:, q, 0:(RCOLS + 1) * BUCKETS].rearrange("p (j b) -> p j b", b=BUCKETS)
                dve.wait_ge(s["ranks_ready"], g + 1)
                dve.tensor_copy(carry[:, 1 - q, :], r[:, RCOLS, :]).then_inc(s["carry_ready"], 1)
                dve.tensor_tensor(ranked[:, q, :, :], r[:, 0:RCOLS, :], onehot[:, q, :, :], ALU.mult).then_inc(s["ranks_picked"], 1)
                dve.wait_ge(s["ranks_picked"], g + 1)
                dve.tensor_reduce(pos[:, bass.ds(g * RCOLS, RCOLS)], ranked[:, q, :, :], AX_X, ALU.add).then_inc(s["positions_ready"], 1)

            make_onehot(0, 0)
            with dve.Fori(0, RGROUPS // 2 - 1) as i:
                make_onehot(i * 2 + 1, 1)
                pick_ranks(i * 2, 0)
                make_onehot(i * 2 + 2, 0)
                pick_ranks(i * 2 + 1, 1)
            make_onehot(RGROUPS - 1, 1)
            pick_ranks(RGROUPS - 2, 0)
            pick_ranks(RGROUPS - 1, 1)

            dve.wait_ge(s["pe_setup"], 2)
            link(dve.tensor_copy(end_col[:], setup_ps[0:BUCKETS, 1, 0:1]))
            dve.tensor_scalar(unit_no[:], unit_no[:], end_col[:, 0:1], None, ALU.is_ge).then_inc(s["dve_setup"], 1)
            HU = UNITS // 2
            dve.wait_ge(s["pe_setup"], 3)
            for k in range(2):
                dve.tensor_scalar(unit_bucket[:, k * HU:(k + 1) * HU], setup_ps[0:1, k, 0:HU], float(BUCKETS - 1), None, ALU.min)
                dve.tensor_scalar(lagged_bucket[:, LAG + k * HU:LAG + (k + 1) * HU], setup_ps[0:1, k, 0:HU], float(BUCKETS - 1), None, ALU.min)

            dve.memset(lagged_bucket[:, 0:LAG], 0)
            dve.memset(lagged_bucket[:, LAG + UNITS:], 0)

            dve.wait_ge(s["params_loaded"], NPAR)
            dve.tensor_scalar(w2s[:], w2raw[:], 0.5, None, ALU.mult)
            link(dve.tensor_copy(bias_p[:, 0, :], bias_f[:]))
            link(dve.tensor_tensor(bias_r[:], bias_f[:], bias_p[:, 0, :], ALU.subtract))
            link(dve.tensor_copy(bias_p[:, 1, :], bias_r[:]))
            link(dve.tensor_tensor(bias_p[:, 2, :], bias_r[:], bias_p[:, 1, :], ALU.subtract))
            link(dve.tensor_scalar(bias_f[:], bias_p[:, 0, :], ident[0:3, 0:1], None, ALU.mult))
            link(dve.scalar_tensor_tensor(bias_r[:], bias_p[:, 1, :], ident[0:3, 1:2], bias_f[:], ALU.mult, ALU.add))
            dve.scalar_tensor_tensor(bparts[:], bias_p[:, 2, :], ident[0:3, 2:3], bias_r[:], ALU.mult, ALU.add).then_inc(s["bias_done"], 1)

            def normaliser(g, k, first):
                c = g * 2 + k
                dve.wait_ge(s["aggregated"], c * NG + NG)
                dve.tensor_scalar(ve[:, k, :], mv[:, k, :, 1], EPS, None, ALU.add).then_inc(s["ve_done"], 1)
                dve.wait_ge(s["sd_done"], c + 1)
                dve.reciprocal(rs[:, k, :], sd[:, k, :]).then_inc(s["small"], 1)
                dve.wait_ge(s["small"], c * 6 + 1)
                dve.tensor_tensor(r2[:, k, :], rs[:, k, :], rs[:, k, :], ALU.mult).then_inc(s["small"], 1)
                dve.wait_ge(s["small"], c * 6 + 2)
                dve.tensor_tensor(r2[:, k, :], r2[:, k, :], ve[:, k, :], ALU.mult).then_inc(s["small"], 1)
                dve.wait_ge(s["small"], c * 6 + 3)
                dve.tensor_scalar(r2[:, k, :], r2[:, k, :], -0.5, 1.5, ALU.mult, ALU.add).then_inc(s["small"], 1)
                dve.wait_ge(s["small"], c * 6 + 4)
                dve.tensor_tensor(rs[:, k, :], rs[:, k, :], r2[:, k, :], ALU.mult).then_inc(s["small"], 1)
                dve.wait_ge(s["small"], c * 6 + 5)
                dve.scalar_tensor_tensor(nb[:, k, :], mv[:, k, :, 0], -1.0, rs[:, k, :], ALU.mult, ALU.mult).then_inc(s["small"], 1)

            def statistics(of, k, c):
                for t in range(NG):
                    dve.bn_stats(stats[:, t, :], of[:, t, :]).then_inc(s["stats_done"], 1)
                dve.wait_ge(s["stats_done"], c * NG + NG)
                dve.sem_inc(s["stats_waited"], 1)
                for t in range(NG):
                    dve.bn_aggr(mv[:, k, t, :], stats[:, t, :]).then_inc(s["aggregated"], 1)

            def nodes(g, q, i):
                dve.wait_ge(s[f"x_loaded{q}"], i * 32 + 32)
                statistics(xg[:, q], 0, g * 2)
                normaliser(g, 0, False)
                dve.wait_ge(s["h_done"], g * NG + NG)
                statistics(hg, 1, g * 2 + 1)
                normaliser(g, 1, False)
                dve.tensor_tensor(xg[:, q], xg[:, q], hg[:], ALU.add).then_inc(s["base_done"], 1)
                dve.wait_ge(s["z_done"], g * NG + NG)
                dve.tensor_tensor(hg[:], hg[:], lnw_b[:].unsqueeze(1).to_broadcast([P, NG, H]), ALU.mult).then_inc(s["lnw_done"], 1)
                dve.wait_ge(s["lnw_done"], g + 1)
                return None

            def xn_of(g):
                dve.tensor_tensor(kvx[:, :, 2 * H:3 * H], hg[:], lnb_b[:].unsqueeze(1).to_broadcast([P, NG, H]), ALU.add).then_inc(s["xn_done"], 1)

            def split_q(g):
                dve.wait_ge(s["q_hi"], g * NG + NG)
                dve.tensor_tensor(qr[:], qf[:], q3[:, :, 0, :], ALU.subtract).then_inc(s["q_rest"], 1)
                dve.wait_ge(s["q_rest"], g + 1)
                dve.tensor_copy(q3[:, :, 1, :], qr[:]).then_inc(s["q_mid"], 1)
                dve.wait_ge(s["q_mid"], g + 1)
                dve.tensor_tensor(q3[:, :, 2, :], qr[:], q3[:, :, 1, :], ALU.subtract).then_inc(s["q_lo"], 1)

            nodes(0, 0, 0)
            xn_of(0)
            split_q(0)
            nodes(1, 1, 0)
            dve.wait_ge(s["table_stored"], 16)
            xn_of(1)
            split_q(1)
            with dve.Fori(1, NGROUPS // 2) as i:
                for q in range(2):
                    nodes(i * 2 + q, q, i)
                    dve.wait_ge(s["table_stored"], i * 32 + 16 * q)
                    xn_of(i * 2 + q)
                    split_q(i * 2 + q)

        @block.tensor
        def _(pe):
            pe.wait_ge(s["dve_setup"], BUCKETS)
            pe.wait_ge(s["consts"], 10)
            pe.matmul(setup_ps[:, 0, 0:BUCKETS], ones_f[:], count[:], start=True, stop=True).then_inc(s["pe_setup"], 1)
            pe.wait_ge(s["carry_ready"], 1)
            pe.transpose(setup_ps[0:BUCKETS, 1, 0:P], end_f[:], ident[:]).then_inc(s["pe_setup"], 1)

            def rank(g, q, reused):
                r = rank_ps[:, q, 0:(RCOLS + 1) * BUCKETS].rearrange("p (j b) -> p j b", b=BUCKETS)
                pe.wait_ge(s["onehot_ready"], g + 1)
                if reused:
                    pe.wait_ge(s["ranks_picked"], g - 1)
                pe.wait_ge(s["carry_ready"], g + 1)
                pe.matmul(r, ident[:], carry[:, q, :].unsqueeze(1).to_broadcast([P, RCOLS + 1, BUCKETS]), start=True, stop=False)
                pe.matmul(r[:, 0:RCOLS, :], tri[:], onehot[:, q, :, :], start=False, stop=False)
                for j in range(RCOLS):
                    n = RCOLS - j
                    m = pe.matmul(r[:, j + 1:RCOLS + 1, :], ones_bf[:], onehot[:, q, j, :].unsqueeze(1).to_broadcast([P, n, BUCKETS]),
                                  start=False, stop=(n == 1))
                m.then_inc(s["ranks_ready"], 1)

            rank(0, 0, False)
            rank(1, 1, False)
            with pe.Fori(1, RGROUPS // 2) as i:
                rank(i * 2, 0, True)
                rank(i * 2 + 1, 1, True)
            HU = UNITS // 2
            pe.wait_ge(s["dve_setup"], BUCKETS + 1)
            for k in range(2):
                m = pe.matmul(setup_ps[0:1, k, 0:HU], ones_f[0:BUCKETS, 0:1], unit_no[:, k * HU:(k + 1) * HU], start=True, stop=True)
            m.then_inc(s["pe_setup"], 1)

            pe.wait_ge(s["bias_done"], 1)
            pe.wait_ge(s["params_loaded"], NPAR)

            def node_tile(c, g, t, first):
                pe.wait_ge(s["xn_done"], g + 1)
                if not first:
                    pe.wait_ge(s["xnt_sb"], c)
                for k in range(2):
                    m = pe.transpose(t_ps[:, k, :], kvx[:, t, 2 * H + k * P:2 * H + (k + 1) * P], ident[:])
                m.then_inc(s["xnt_ps"], 1)
                pe.wait_ge(s["xnt_sb"], c + 1)
                if not first:
                    pe.wait_ge(s["kv_out"], c)
                pe.matmul(kv_ps[:, 0:2 * H], ones_bf[0:3, :], bparts[:, BKV], start=True, stop=False)
                for k in range(2):
                    m = pe.matmul(kv_ps[:, 0:2 * H], xnT[:, 0, k, :], wkvs[:, k, :], start=False, stop=(k == 1))
                m.then_inc(s["kv_done"], 1)
                if not first:
                    pe.wait_ge(s["q_out"], c)
                pe.matmul(q_ps[:, 0:H], ones_bf[0:3, :], bparts[:, BQ], start=True, stop=False)
                for k in range(2):
                    m = pe.matmul(q_ps[:, 0:H], xnT[:, 0, k, :], wqs[:, k, :], start=False, stop=(k == 1))
                m.then_inc(s["q_done"], 1)

            for t in range(NG):
                node_tile(t, 0, t, t == 0)
            with pe.Fori(1, NGROUPS) as g:
                for t in range(NG):
                    node_tile(g * NG + t, g, t, False)

        @block.scalar
        def _(act):
            def root(c, k):
                act.wait_ge(s["ve_done"], c + 1)
                act.activation(sd[:, k, :], ve[:, k, :], ACT.Sqrt).then_inc(s["sd_done"], 1)

            def node_scalar(g):
                q = g % 2
                root(2 * g, 0)
                act.wait_ge(s["small"], 12 * g + 6)
                if g >= 1:
                    act.wait_ge(s["xn_done"], g)
                for t in range(NG):
                    act.activation(hg[:, t, :], xg[:, q, t, :], ACT.Relu, bias=nb[:, 0, t:t + 1], scale=rs[:, 0, t:t + 1]).then_inc(s["h_done"], 1)
                root(2 * g + 1, 1)
                act.wait_ge(s["small"], 12 * g + 12)
                act.wait_ge(s["base_done"], g + 1)
                act.dma_start(base[g * NG * P:(g + 1) * NG * P, :].rearrange("(t p) f -> p t f", p=P), xg[:, q]).then_inc(s["base_stored"], 16)
                for t in range(NG):
                    act.activation(hg[:, t, :], hg[:, t, :], ACT.Identity, bias=nb[:, 1, t:t + 1], scale=rs[:, 1, t:t + 1]).then_inc(s["z_done"], 1)
                if g + 2 < NGROUPS:
                    act.wait_ge(s["base_stored"], 16 * (g + 1))
                    load_x(g + 2)
                for t in range(NG):
                    c = g * NG + t
                    act.wait_ge(s["xnt_ps"], c + 1)
                    if c >= 1:
                        act.wait_ge(s["q_done"], c)
                    act.activation(xnT[:, 0, :, :], t_ps[:], ACT.Copy).then_inc(s["xnt_sb"], 1)
                    act.wait_ge(s["kv_done"], c + 1)
                    act.activation(kvx[:, t, 0:H], kv_ps[:, 0:H], ACT.Copy)
                    act.activation(kvx[:, t, H:2 * H], kv_ps[:, H:2 * H], ACT.Copy, scale=gate_b[:, 0:1]).then_inc(s["kv_out"], 1)
                    act.wait_ge(s["q_done"], c + 1)
                    if t == 0 and g >= 1:
                        act.wait_ge(s["q_lo"], g)
                        act.wait_ge(s["q_stored"], 16 * g)
                    act.activation(qf[:, t, :], q_ps[:, 0:H], ACT.Copy).then_inc(s["q_out"], 1)
                    act.wait_ge(s["q_out"], c + 1)
                    act.activation(q3[:, t, 0, :], qf[:, t, :], ACT.Copy).then_inc(s["q_hi"], 1)
                act.wait_ge(s["kv_out"], (g + 1) * NG)
                act.dma_start(table[g * NG * P:(g + 1) * NG * P, :].rearrange("(t p) f -> p t f", p=P), kvx[:]).then_inc(s["table_stored"], 16)
                act.wait_ge(s["q_lo"], g + 1)
                act.dma_start(qparts[g * NG * P:(g + 1) * NG * P, :].rearrange("(t p) f -> p t f", p=P),
                              q3[:].rearrange("p t k f -> p t (k f)")).then_inc(s["q_stored"], 16)

            def load_x(g):
                q = g % 2
                rows = x[g * NG * P:min((g + 1) * NG * P, N), :]
                if g < NGROUPS - 1:
                    half = NG // 2
                    for a, b in ((0, half), (half, NG)):
                        act.dma_start(xg[:, q, a:b, :], rows[a * P:b * P, :].rearrange("(t p) f -> p t f", p=P)).then_inc(s[f"x_loaded{q}"], 16)
                    return
                act.activation(xg[:, q, NG - 1, :], xg[:, q, NG - 1, :], ACT.Copy, scale=0.0).then_inc(s["stored"], 1)
                act.wait_ge(s["stored"], 1)
                act.dma_start(xg[:, q, 0:NG - 1, :], rows[0:(NG - 1) * P, :].rearrange("(t p) f -> p t f", p=P)).then_inc(s[f"x_loaded{q}"], 16)
                act.dma_start(xg[0:LAST_ROWS, q, NG - 1, :], rows[(NG - 1) * P:, :]).then_inc(s[f"x_loaded{q}"], 16)

            load_x(0)
            load_x(1)
            act.wait_ge(s["params_loaded"], NPAR)
            for g in range(NGROUPS):
                node_scalar(g)
            act.wait_ge(s["base_stored"], 16 * NGROUPS)
            act.wait_ge(s["table_stored"], 16 * NGROUPS)
            act.wait_ge(s["q_stored"], 16 * NGROUPS)


def edges(nc, sb_, sem, recs, table, qparts, ident, ones_bf, iota1, w1s, w2s, bparts, unit_bucket, lagged_bucket, aggr, B2):
    with ExitStack() as st:
        def sb(name, shape, dt=F32):
            return st.enter_context(nc.sbuf_tensor(name, shape, dt))

        def ps(name, shape, dt=F32):
            return st.enter_context(nc.psum_tensor(name, shape, dt))

        rec = sb("urec", [P, DEPTH, 2, REC])
        dst_i = sb("udst", [P, DEPTH, 2], I32)
        qb = sb("uq", [P, DEPTH, 3, H], BF16)
        kvx = sb("ukvx", [P, KVDEPTH, 2, TAB])
        oh = sb("uonehot", [P, OHDEPTH, 2, P])
        away = sb("uaway", [P, 2, 2, P])
        ohT = sb("uonehotT", [P, 2, 2, P], BF16)
        rT = sb("urT", [NRBF + 1, 2, 2 * P])
        th = sb("utanh", [P, 2, 2, UNIT])
        hid = sb("uhid", [P, 2, 2, UNIT])
        prod = sb("uprod", [P, 2, 2 * NH, HD])
        sc = sb("uscores", [P, 2, 2, NH])
        mx = sb("umax", [P, 2, 2])
        ex = sb("uexp", [P, 2, 2, NH])
        sm = sb("usum", [P, 2, 2])
        rc = sb("urecip", [P, 2, 2])
        av = sb("uav", [P, 2, 2, H])
        phys = sb("uphys", [P, 2, 2, H])
        msg = sb("umsg", [P, 2, 2, H])
        turn_ps = [ps(f"turn_ps{k}", [P, 4, P]) for k in range(2)]
        hid_ps = [ps(f"hid_ps{k}", [P, 2, UNIT]) for k in range(2)]
        q_ps = ps("uq_ps", [P, 2, H])
        w_ps = ps("w_ps", [P, 2, H])
        ag_ps = [ps(f"ag_ps{k}", [P, 512]) for k in range(2)]

        s = {n: sem("u_" + n) for n in (
            "zeroed", "dst_ready", "dst_waited", "away_ready", "onehot_ready", "turned", "rT_ready", "hid_done", "qe_done", "tanh_ready",
            "hid_ready", "w_done", "qk_done", "scored", "weighted", "max_done", "exp_ready",
            "recip_done", "av_done", "phys_done", "msg_ready", "ag_done", "ag_added")}
        rec_in = [sem(f"u_rec_in{k}") for k in range(DEPTH)]
        q_in = [sem(f"u_q_in{k}") for k in range(DEPTH)]
        kvx_in = [sem(f"u_kvx_in{k}") for k in range(KVDEPTH)]
        TURNS = UNITS // DEPTH
        GATHER_AHEAD = 2
        rec_v = recs.rearrange("(u p j) f -> u p j f", p=P, j=2)
        q_v = qparts.rearrange("(b p) f -> b p f", p=P)

        def turns(eng, body):
            for k in range(DEPTH):
                body(k, k, 0, True, False)
            with eng.Fori(1, TURNS - 1) as i:
                for k in range(DEPTH):
                    body(i * DEPTH + k, k, i, False, False)
            for k in range(DEPTH):
                body((TURNS - 1) * DEPTH + k, k, TURNS - 1, False, True)

        block = st.enter_context(nc.Block())

        @block.sync
        def _(sp):
            bucket_of = [None] * DEPTH

            def unit(u, k, i, first, last):
                if k == 0:
                    _, bucket_of[:] = nc.values_load_multi_w_load_instructions(
                        unit_bucket[0:1, bass.ds(u, DEPTH)], engines=[mybir.EngineType.SP], min_val=0, max_val=BUCKETS - 1)
                if not first:
                    sp.wait_ge(s["av_done"], u - (DEPTH - 1))
                    sp.wait_ge(s["phys_done"], u - (DEPTH - 1))
                sp.dma_start(rec[:, k], rec_v[u] if isinstance(u, int) else rec_v[bass.ds(u, 1)].rearrange("a p j f -> p (a j) f")).then_inc(rec_in[k], 16)
                b = bucket_of[k]
                sp.dma_start(qb[:, k], q_v[bass.ds(b, 1)].rearrange("a p (k f) -> p (a k) f", k=3)).then_inc(q_in[k], 16)
            turns(sp, unit)

        @block.gpsimd
        def _(pool):
            def gather(u, k, i, first):
                if not (first and k < KVDEPTH):
                    pool.wait_ge(s["av_done"], u - (KVDEPTH - 1))
                    pool.wait_ge(s["phys_done"], u - (KVDEPTH - 1))
                pool.wait_ge(s["dst_ready"], u + 1)
                pool.sem_inc(s["dst_waited"], 1)
                for j in range(2):
                    pool.indirect_dma_start(kvx[:, k % KVDEPTH, j, :], None, table,
                                            bass.IndirectOffsetOnAxis(ap=dst_i[:, k, j:j + 1], axis=0)).then_inc(kvx_in[k % KVDEPTH], 16)

            def sum_up(u, k, i, first):
                q = k % 2
                pool.wait_ge(s["phys_done"], u + 1)
                pool.wait_ge(s["av_done"], u + 1)
                if not (first and k < 2):
                    pool.wait_ge(s["ag_done"], u - 1)
                pool.tensor_tensor(msg[:, q], phys[:, q], av[:, q], ALU.add).then_inc(s["msg_ready"], 1)

            for k in range(GATHER_AHEAD):
                gather(k, k, 0, True)

            def unit(u, k, i, first, last):
                if not (last and k + GATHER_AHEAD >= DEPTH):
                    k2, wrap = (k + GATHER_AHEAD) % DEPTH, (k + GATHER_AHEAD) // DEPTH
                    gather(u + GATHER_AHEAD, k2, i + wrap, first and not wrap)
                if not (first and k < 1):
                    sum_up(u - 1, (k - 1) % DEPTH, i - (k < 1), first)
            turns(pool, unit)
            sum_up(UNITS - 1, DEPTH - 1, TURNS - 1, False)

        @block.scalar
        def _(act):
            def destinations(u, k, i):
                act.wait_ge(rec_in[k], i * 16 + 16)
                act.activation(dst_i[:, k, :], rec[:, k, :, R_DST], ACT.Copy).then_inc(s["dst_ready"], 1)

            def select(u, k, i, first):
                q = k % 2
                act.wait_ge(rec_in[k], i * 16 + 16)
                if not (first and k < OHDEPTH):
                    act.wait_ge(s["ag_done"], u - (OHDEPTH - 1))
                for j in range(2):
                    m = act.activation(away[:, q, j, :], iota1[:], ACT.Abs, bias=rec[:, k, j, R_LOC:R_LOC + 1])
                m.then_inc(s["away_ready"], 1)
                act.wait_ge(s["away_ready"], u + 1)
                act.activation(oh[:, k % OHDEPTH], away[:, q], ACT.Relu, bias=1.0, scale=-1.0).then_inc(s["onehot_ready"], 1)

            def evacuate(u, k, i, first):
                q = k % 2
                act.wait_ge(s["turned"], u + 1)
                if not (first and k < 2):
                    act.wait_ge(s["qe_done"], u - 1)
                act.activation(rT[:, q, :].rearrange("p (j e) -> p j e", j=2), turn_ps[q][0:NRBF + 1, 0:2, :], ACT.Copy)
                act.activation(ohT[:, q], turn_ps[q][:, 2:4, :], ACT.Copy).then_inc(s["rT_ready"], 1)

            def tanh(u, k, i, first):
                q = k % 2
                act.wait_ge(s["hid_done"], u + 1)
                if not (first and k < 2):
                    act.wait_ge(s["hid_ready"], u - 1)
                act.activation(th[:, q], hid_ps[q][:], ACT.Tanh, scale=0.5).then_inc(s["tanh_ready"], 1)

            def exponent(u, k, i, first):
                q = k % 2
                act.wait_ge(s["max_done"], u + 1)
                if not (first and k < 2):
                    act.wait_ge(s["av_done"], u - 1)
                for j in range(2):
                    m = act.activation(ex[:, q, j, :], sc[:, q, j, :], ACT.Exp, bias=mx[:, q, j:j + 1], accum_out=sm[:, q, j:j + 1])
                m.then_inc(s["exp_ready"], 1)

            for k in range(GATHER_AHEAD):
                destinations(k, k, 0)
            select(0, 0, 0, True)
            select(1, 1, 0, True)
            evacuate(0, 0, 0, True)

            def unit(u, k, i, first, last):
                if not (last and k + 1 >= DEPTH):
                    evacuate(u + 1, (k + 1) % DEPTH, i + (k + 1) // DEPTH, first and k + 1 < DEPTH)
                tanh(u, k, i, first)
                if not (first and k < 1):
                    exponent(u - 1, (k - 1) % DEPTH, i - (k < 1), first and k < 3)
                if not (last and k + GATHER_AHEAD >= DEPTH):
                    destinations(u + GATHER_AHEAD, (k + GATHER_AHEAD) % DEPTH, i + (k + GATHER_AHEAD) // DEPTH)
                if not (last and k + 2 >= DEPTH):
                    select(u + 2, (k + 2) % DEPTH, i + (k + 2) // DEPTH, first and k + 2 < DEPTH)
            turns(act, unit)
            exponent(UNITS - 1, DEPTH - 1, TURNS - 1, False)

        @block.tensor
        def _(pe):
            def turn(u, k, i, first):
                q = k % 2
                pe.wait_ge(rec_in[k], i * 16 + 16)
                pe.wait_ge(s["onehot_ready"], u + 1)
                if not (first and k < 2):
                    pe.wait_ge(s["rT_ready"], u - 1)
                for j in range(2):
                    pe.transpose(turn_ps[q][0:NRBF + 1, j, :], rec[:, k, j, 0:NRBF + 1], ident[:])
                for j in range(2):
                    m = pe.transpose(turn_ps[q][:, 2 + j, :], oh[:, k % OHDEPTH, j, :], ident[:])
                m.then_inc(s["turned"], 1)

            def hidden_and_q(u, k, i, first):
                q = k % 2
                pe.wait_ge(s["rT_ready"], u + 1)
                if not (first and k < 2):
                    pe.wait_ge(s["hid_ready"], u - 1)
                for c in range(2):
                    m = pe.matmul(hid_ps[q][:, c, :], w1s[:, c * P:(c + 1) * P], rT[:, q, :], start=(c == 0), stop=True, skip_group_check=True)
                m.then_inc(s["hid_done"], 1)
                pe.wait_ge(q_in[k], i * 16 + 16)
                if not (first and k < 1):
                    pe.wait_ge(s["qk_done"], u)
                for j in range(2):
                    for part in range(3):
                        m = pe.matmul(q_ps[:, j, :], ohT[:, q, j, :], qb[:, k, part, :], start=(j == 0 and part == 0), stop=(part == 2), skip_group_check=True)
                m.then_inc(s["qe_done"], 1)

            def filters(u, k, i, first):
                q = k % 2
                pe.wait_ge(s["hid_ready"], u + 1)
                if not (first and k < 1):
                    pe.wait_ge(s["phys_done"], u)
                for j in range(2):
                    pe.matmul(w_ps[:, j, :], ones_bf[0:3, :], bparts[:, B2], start=(j == 0), stop=False, skip_group_check=True)
                    for c in range(2):
                        m = pe.matmul(w_ps[:, j, :], hid[:, q, c, j * P:(j + 1) * P], w2s[:, c, :], start=False, stop=(c == 1), skip_group_check=True)
                m.then_inc(s["w_done"], 1)

            def aggregate(u, k, i, first):
                q = k % 2
                pe.wait_ge(s["msg_ready"], u + 1)
                if not first:
                    pe.wait_ge(s["ag_added"], u - 1)
                for j in range(2):
                    m = pe.matmul(ag_ps[q][:, 0:H], oh[:, k % OHDEPTH, j, :], msg[:, q, j, :], start=(j == 0), stop=(j == 1))
                m.then_inc(s["ag_done"], 1)

            turn(0, 0, 0, True)

            def unit(u, k, i, first, last):
                if not (last and k + 1 >= DEPTH):
                    turn(u + 1, (k + 1) % DEPTH, i + (k + 1) // DEPTH, first and k + 1 < DEPTH)
                hidden_and_q(u, k, i, first)
                if not (first and k < 1):
                    filters(u - 1, (k - 1) % DEPTH, i - (k < 1), first)
                if not (first and k < 2):
                    aggregate(u - 2, (k - 2) % DEPTH, i - (k < 2), first and k < 4)
            turns(pe, unit)
            U = UNITS
            filters(U - 1, DEPTH - 1, TURNS - 1, False)
            aggregate(U - 2, DEPTH - 2, TURNS - 1, False)
            aggregate(U - 1, DEPTH - 1, TURNS - 1, False)

        @block.vector
        def _(dve):
            dve.memset(aggr[:], 0.0).then_inc(s["zeroed"], 1)
            dve.wait_ge(s["zeroed"], 1)

            def query_key(u, k, i, first):
                q = k % 2
                dve.wait_ge(s["qe_done"], u + 1)
                dve.wait_ge(kvx_in[k % KVDEPTH], i * (32 * DEPTH // KVDEPTH) + 32 * (k // KVDEPTH + 1))
                if not (first and k < 2):
                    dve.wait_ge(s["scored"], u - 1)
                dve.tensor_tensor(prod[:, q].rearrange("p (j h) d -> p j (h d)", j=2), q_ps[:], kvx[:, k % KVDEPTH, :, 0:H], ALU.mult).then_inc(s["qk_done"], 1)

            def silu(u, k, i, first):
                q = k % 2
                dve.wait_ge(s["tanh_ready"], u + 1)
                if not (first and k < 2):
                    dve.wait_ge(s["w_done"], u - 1)
                dve.scalar_tensor_tensor(hid[:, q], th[:, q], 1.0, hid_ps[q][:], ALU.add, ALU.mult).then_inc(s["hid_ready"], 1)

            def score(u, k, i, first):
                q = k % 2
                dve.wait_ge(s["qk_done"], u + 1)
                if not (first and k < 2):
                    dve.wait_ge(s["exp_ready"], u - 1)
                dve.tensor_reduce(sc[:, q].rearrange("p j h -> p (j h)"), prod[:, q], AX_X, ALU.add).then_inc(s["scored"], 1)

            def weigh(u, k, i, first):
                q = k % 2
                dve.wait_ge(s["scored"], u + 1)
                dve.scalar_tensor_tensor(sc[:, q], sc[:, q], float(HD) ** -0.5, rec[:, k, :, R_W:R_W + 1].to_broadcast([P, 2, NH]), ALU.mult, ALU.mult).then_inc(s["weighted"], 1)

            def maximum(u, k, i, first):
                q = k % 2
                dve.wait_ge(s["weighted"], u + 1)
                dve.tensor_reduce(mx[:, q], sc[:, q], AX_X, ALU.max, negate=True).then_inc(s["max_done"], 1)

            def invert(u, k, i, first):
                q = k % 2
                dve.wait_ge(s["exp_ready"], u + 1)
                if not (first and k < 2):
                    dve.wait_ge(s["av_done"], u - 1)
                dve.reciprocal(rc[:, q], sm[:, q]).then_inc(s["recip_done"], 1)

            def filtered(u, k, i, first):
                q = k % 2
                dve.wait_ge(s["w_done"], u + 1)
                if not (first and k < 2):
                    dve.wait_ge(s["msg_ready"], u - 1)
                for j in range(2):
                    m = dve.scalar_tensor_tensor(phys[:, q, j, :], w_ps[:, j, :], rec[:, k, j, R_W:R_W + 1], kvx[:, k % KVDEPTH, j, 2 * H:3 * H], ALU.mult, ALU.mult)
                m.then_inc(s["phys_done"], 1)

            def attend(u, k, i, first):
                q = k % 2
                dve.wait_ge(s["recip_done"], u + 1)
                if not (first and k < 2):
                    dve.wait_ge(s["msg_ready"], u - 1)
                for j in range(2):
                    m = dve.scalar_tensor_tensor(av[:, q, j, :].rearrange("p (h d) -> p h d", h=NH), kvx[:, k % KVDEPTH, j, H:2 * H].rearrange("p (h d) -> p h d", h=NH),
                                                 rc[:, q, j:j + 1], ex[:, q, j, :].unsqueeze(2).to_broadcast([P, NH, HD]), ALU.mult, ALU.mult)
                m.then_inc(s["av_done"], 1)

            def add_up(u, q, b, first):
                dve.wait_ge(s["ag_done"], u + 1)
                if not first:
                    dve.wait_ge(s["ag_added"], u)
                row = aggr[:, bass.ds(b, 1), :].rearrange("p a f -> p (a f)")
                dve.tensor_tensor(row, row, ag_ps[q][:, 0:H], ALU.add).then_inc(s["ag_added"], 1)

            bucket_of = [None] * DEPTH

            def unit(u, k, i, first, last):
                if k == 0:
                    _, bucket_of[:] = nc.values_load_multi_w_load_instructions(
                        lagged_bucket[0:1, 0:DEPTH] if first else lagged_bucket[0:1, bass.ds(u, DEPTH)],
                        engines=[mybir.EngineType.DVE], min_val=0, max_val=BUCKETS - 1)
                silu(u, k, i, first)
                query_key(u, k, i, first)
                if not (first and k < LAG):
                    add_up(u - LAG, (k - LAG) % 2, bucket_of[k], first and k == LAG)
                score(u, k, i, first)
                if not (first and k < 1):
                    before = (u - 1, (k - 1) % DEPTH, i - (k < 1), first)
                    invert(*before)
                weigh(u, k, i, first)
                if not (first and k < 1):
                    filtered(*before)
                maximum(u, k, i, first)
                if not (first and k < 1):
                    attend(*before)
            turns(dve, unit)
            U = UNITS
            before = (U - 1, DEPTH - 1, TURNS - 1, False)
            invert(*before)
            filtered(*before)
            attend(*before)
            _, rest = nc.values_load_multi_w_load_instructions(lagged_bucket[0:1, UNITS:UNITS + DEPTH], engines=[mybir.EngineType.DVE], min_val=0, max_val=BUCKETS - 1)
            for n in range(LAG):
                add_up(U - LAG + n, (U - LAG + n) % 2, rest[n], False)


def finish(nc, sb_, sem, base, out, ident, ones_bf, wos, bparts, aggr, BO):
    with ExitStack() as st:
        def sb(name, shape, dt=F32):
            return st.enter_context(nc.sbuf_tensor(name, shape, dt))

        def ps(name, shape, dt=F32):
            return st.enter_context(nc.psum_tensor(name, shape, dt))

        ag = sb("fag", [P, 2, H])
        agT = sb("fagT", [P, 2, 2, P])
        bs = sb("fbase", [P, 2, H])
        ot = sb("fout", [P, 2, H])
        t_ps = [ps(f"ft_ps{k}", [P, 4, P]) for k in range(2)]
        o_ps = [ps(f"fo_ps{k}", [P, 512]) for k in range(2)]
        s = {n: sem("f_" + n) for n in ("copied", "turned", "turned_out", "projected", "summed")}
        base_in = [sem(f"f_base_in{k}") for k in range(2)]
        stored = [sem(f"f_stored{k}") for k in range(2)]
        base_v = base.rearrange("(b p) f -> b p f", p=P)
        out_v = out[0:(BUCKETS - 1) * P, :].rearrange("(b p) f -> b p f", p=P)
        HALF = BUCKETS // 2
        block = st.enter_context(nc.Block())

        @block.sync
        def _(sp):
            for q in range(2):
                sp.dma_start(bs[:, q], base_v[q]).then_inc(base_in[q], 16)
            with sp.Fori(1, HALF) as i:
                for q in range(2):
                    sp.wait_ge(s["summed"], i * 2 + q - 1)
                    sp.dma_start(bs[:, q], base_v[bass.ds(i * 2 + q, 1)].rearrange("a p f -> p (a f)")).then_inc(base_in[q], 16)

        @block.gpsimd
        def _(pool):
            def store(b, q):
                pool.wait_ge(s["summed"], b + 1)
                pool.dma_start(out_v[bass.ds(b, 1)].rearrange("a p f -> p (a f)"), ot[:, q]).then_inc(stored[q], 16)
            with pool.Fori(0, HALF - 1) as i:
                for q in range(2):
                    store(i * 2 + q, q)
            pool.wait_ge(s["summed"], BUCKETS - 1)
            pool.dma_start(out_v[BUCKETS - 2], ot[:, 0]).then_inc(stored[0], 16)
            pool.wait_ge(s["summed"], BUCKETS)
            pool.dma_start(out[(BUCKETS - 1) * P:N, :], ot[0:LAST_ROWS, 1]).then_inc(stored[1], 16)
            for q in range(2):
                pool.wait_ge(stored[q], 16 * HALF)

        @block.scalar
        def _(act):
            def tile(b, q, first):
                act.wait_ge(s["turned"], b + 1)
                if not first:
                    act.wait_ge(s["projected"], b - 1)
                act.activation(agT[:, q], t_ps[q][:, 0:2, :], ACT.Copy).then_inc(s["turned_out"], 1)
            for q in range(2):
                tile(q, q, True)
            with act.Fori(1, HALF) as i:
                for q in range(2):
                    tile(i * 2 + q, q, False)

        @block.tensor
        def _(pe):
            def tile(b, q, first):
                pe.wait_ge(s["copied"], b + 1)
                if not first:
                    pe.wait_ge(s["turned_out"], b - 1)
                for c in range(2):
                    m = pe.transpose(t_ps[q][:, c, :], ag[:, q, c * P:(c + 1) * P], ident[:])
                m.then_inc(s["turned"], 1)
                pe.wait_ge(s["turned_out"], b + 1)
                if not first:
                    pe.wait_ge(s["summed"], b - 1)
                pe.matmul(o_ps[q][:, 0:H], ones_bf[0:3, :], bparts[:, BO], start=True, stop=False)
                for c in range(2):
                    m = pe.matmul(o_ps[q][:, 0:H], agT[:, q, c, :], wos[:, c, :], start=False, stop=(c == 1))
                m.then_inc(s["projected"], 1)
            for q in range(2):
                tile(q, q, True)
            with pe.Fori(1, HALF) as i:
                for q in range(2):
                    tile(i * 2 + q, q, False)

        @block.vector
        def _(dve):
            def copy(b, q, first):
                if not first:
                    dve.wait_ge(s["turned"], b - 1)
                dve.tensor_copy(ag[:, q], aggr[:, b, :] if first else aggr[:, bass.ds(b, 1), :].rearrange("p a f -> p (a f)")).then_inc(s["copied"], 1)

            def total(b, q, i, first):
                dve.wait_ge(s["projected"], b + 1)
                dve.wait_ge(base_in[q], i * 16 + 16)
                if not first:
                    dve.wait_ge(stored[q], i * 16)
                dve.tensor_tensor(ot[:, q], o_ps[q][:, 0:H], bs[:, q], ALU.add).then_inc(s["summed"], 1)
            for q in range(2):
                copy(q, q, True)
            for q in range(2):
                total(q, q, 0, True)
            with dve.Fori(1, HALF) as i:
                for q in range(2):
                    copy(i * 2 + q, q, False)
                for q in range(2):
                    total(i * 2 + q, q, i, False)


_INS = ["x", "src", "dst", "edge_attr_64", "edge_weight", "L0_gnn_w1", "L0_gnn_b1", "L0_gnn_w2", "L0_gnn_b2", "L0_gnn_ln_w",
        "L0_gnn_ln_b", "L0_gnn_wq", "L0_gnn_bq", "L0_gnn_wk", "L0_gnn_bk", "L0_gnn_wv", "L0_gnn_bv", "L0_gnn_wo", "L0_gnn_bo",
        "L0_gnn_gate"]


def kernel(**inputs):
    import numpy as _np
    import concourse.bacc as _bacc
    from concourse import mybir as _mybir
    from concourse.bass_utils import run_bass_kernel_spmd as _run

    nc = _bacc.Bacc("TRN2", target_bir_lowering=False, num_devices=1)
    arrays, args = {}, []
    for name in _INS:
        a = _np.ascontiguousarray(inputs[name])
        arrays[f"in_{name}"] = a
        args.append(nc.dram_tensor(f"in_{name}", a.shape, _mybir.dt.from_np(a.dtype), kind="ExternalInput").ap())
    args.append(nc.dram_tensor("out", (N, H), F32, kind="ExternalOutput").ap())
    build(nc, *args)
    r = _run(nc, [arrays], core_ids=[0])
    return r.results[0]["out"]
```

```python
from contextlib import ExitStack

import concourse.bass as bass
from concourse import mybir

F32 = mybir.dt.float32
F32R = mybir.dt.float32r
BF16 = mybir.dt.bfloat16
I32 = mybir.dt.int32
ALU = mybir.AluOpType
ACT = mybir.ActivationFunctionType
AX_X = mybir.AxisListType.X

P = 128
N = 12500
E = 212500
H = 256
NH, HD = 8, 32
NRBF = 64
EPS = 1e-5
BUCKETS = -(-N // P)
NPAD = BUCKETS * P
LAST_ROWS = N - (BUCKETS - 1) * P
COLS = E // P
TAIL = E - COLS * P
RCOLS = 4
RGROUPS = -(-(COLS + 1) // RCOLS)
CPAD = RGROUPS * RCOLS
NOBUCKET = 200
SCOLS = 20
SGROUPS = COLS // SCOLS
SHIFT = 7
UNIT = 2 * P
USHIFT = 8
OHBDEPTH = 4
OHDEPTH = 8
LAG = 4
DEPTH = 8
QDEPTH = 4
MDEPTH = 4
KVDEPTH = 4
UNITS = -(-((E + BUCKETS * (UNIT - 1)) // UNIT) // DEPTH) * DEPTH
SLOTS = UNITS * UNIT
REC = NRBF + 4
R_ONE, R_W, R_DST, R_LOC = NRBF, NRBF + 1, NRBF + 2, NRBF + 3
TAB = 3 * H
NG = 7
NGROUPS = BUCKETS // NG
ZROWS = 16
ZPIECES = UNIT // ZROWS
FULL = E // UNIT
RBUFS = 2
RTURNS, RREST = divmod(COLS // SCOLS, RBUFS)
VBUCKETS = 58


def build(nc, x, src, dst, rbf, weight, w1, b1, w2, b2, ln_w, ln_b, wq, bq, wk, bk, wv, bv, wo, bo, gate, out):
    recs = nc.dram_tensor("records", [SLOTS, REC], F32).ap()
    table = nc.dram_tensor("kvx_table", [NPAD, TAB], F32).ap()
    queries = nc.dram_tensor("query_table", [NPAD, H], F32).ap()
    base = nc.dram_tensor("x_plus_h", [NPAD, H], F32).ap()
    with ExitStack() as ctx:
        def sb(name, shape, dt, stack=ctx):
            return stack.enter_context(nc.sbuf_tensor(name, shape, dt))

        def sem(name):
            return ctx.enter_context(nc.semaphore(name))

        ident = sb("ident", [P, P], F32)
        ones_bf = sb("ones_bf", [P, P], BF16)
        iota1 = sb("iota1", [P, P], F32)
        w1s = sb("w1s", [NRBF + 1, H], F32)
        w2s = sb("w2s", [P, 2, H], F32)
        wos = sb("wos", [P, 2, H], F32)
        bparts = sb("bparts", [3, 6 * H], BF16)
        unit_bucket = sb("unit_bucket", [1, UNITS], I32)
        lagged_bucket = sb("lagged_bucket", [1, UNITS + DEPTH], I32)
        BQ, BK, BV, B2, BO = (slice(k * H, (k + 1) * H) for k in (0, 1, 2, 3, 4))
        BKV = slice(H, 3 * H)

        prep(nc, sem, x, src, dst, rbf, weight, w1, b1, w2, b2, ln_w, ln_b, wq, bq, wk, bk, wv, bv, wo, bo,
             gate, recs, table, queries, base, ident, ones_bf, iota1, w1s, w2s, wos, bparts, unit_bucket, lagged_bucket, BQ, BKV)
        aggr = sb("aggr", [P, BUCKETS, H], F32)
        edges(nc, sem, recs, table, queries, ident, ones_bf, iota1, w1s, w2s, bparts, unit_bucket, lagged_bucket, aggr, B2)
        finish(nc, sem, base, out, ident, ones_bf, wos, bparts, aggr, BO)


def prep(nc, sem, x, src, dst, rbf, weight, w1, b1, w2, b2, ln_w, ln_b, wq, bq, wk, bk, wv, bv, wo, bo,
         gate, recs, table, queries, base, ident, ones_bf, iota1, w1s, w2s, wos, bparts, unit_bucket, lagged_bucket, BQ, BKV):
    with ExitStack() as st:
        def sb(name, shape, dt):
            return st.enter_context(nc.sbuf_tensor(name, shape, dt))

        def ps(name, shape, dt=F32):
            return st.enter_context(nc.psum_tensor(name, shape, dt))

        src_i = sb("src_i", [P, CPAD], I32)
        dst_i = sb("dst_i", [P, CPAD], I32)
        wgt = sb("wgt", [P, CPAD], F32)
        bucket = sb("bucket", [P, CPAD], BF16)
        meta = sb("meta", [P, CPAD, 4], F32)
        pos = sb("pos", [P, CPAD], I32)
        eq = sb("eq", [P, 2, CPAD], BF16)
        bucket_ids = sb("bucket_ids", [P, BUCKETS], F32)
        bucket_ids_bf = sb("bucket_ids_bf", [P, BUCKETS], BF16)
        tri = sb("tri", [P, P], BF16)
        ones_f = sb("ones_f", [P, P], F32)
        count = sb("count", [P, BUCKETS], F32)
        cut = sb("cut", [P, BUCKETS + 1], F32)
        above = sb("above", [P, BUCKETS + 1], F32)
        piece = sb("piece", [P, ZPIECES], F32)
        last_unit = sb("last_unit", [BUCKETS, 1], F32)
        last_piece = sb("last_piece", [BUCKETS, ZPIECES], I32)
        zero98 = sb("zero98", [P, BUCKETS], F32)
        units_i = sb("units_i", [P, BUCKETS], I32)
        units_f = sb("units_f", [P, BUCKETS], F32)
        end_f = sb("end_f", [P, BUCKETS], F32)
        end_col = sb("end_col", [BUCKETS, 1], F32)
        unit_no = sb("unit_no", [BUCKETS, UNITS], F32)
        carry = sb("carry", [P, 2, BUCKETS], F32)
        onehot = sb("onehot", [P, 2, RCOLS, BUCKETS], BF16)
        ranked = sb("ranked", [P, 2, RCOLS, BUCKETS], F32)
        rec = sb("rec", [P, RBUFS, SCOLS, REC], F32)
        slot_i = sb("slot_i", [P, RBUFS, SCOLS], I32)
        tail_rec = sb("tail_rec", [P, REC], F32)
        tail_slot = sb("tail_slot", [P, 1], I32)
        zero = sb("zero", [P, ZROWS * REC], F32)
        bias_f = sb("bias_f", [3, 6 * H], F32)
        bias_r = sb("bias_r", [3, 6 * H], F32)
        bias_p = sb("bias_p", [3, 3, 6 * H], BF16)
        w2raw = sb("w2raw", [P, 2, H], F32)
        wqs = sb("wqs", [P, 2, H], F32)
        wkvs = sb("wkvs", [P, 2, 2 * H], F32)
        lnw_b = sb("lnw_b", [P, H], F32)
        lnb_b = sb("lnb_b", [P, H], F32)
        gate_b = sb("gate_b", [P, 1], F32)
        xg = sb("xg", [P, 2, NG, H], F32)
        hg = sb("hg", [P, NG, H], F32)
        stats = sb("stats", [P, NG, 6], F32)
        mv = sb("mv", [P, 2, NG, 2], F32)
        ve = sb("ve", [P, 2, NG], F32)
        sd = sb("sd", [P, 2, NG], F32)
        rs = sb("rs", [P, 2, NG], F32)
        r2 = sb("r2", [P, 2, NG], F32)
        nb = sb("nb", [P, 2, NG], F32)
        kvx = sb("kvx", [P, NG, TAB], F32)
        qf = sb("qf", [P, NG, H], F32)
        xnT = sb("xnT", [P, 2, P], F32)

        rank_ps = ps("rank_ps", [P, 2, 512])
        setup_ps = ps("setup_ps", [P, 2, 512])
        t_ps = ps("t_ps", [P, 2, P])
        kv_ps = ps("kv_ps", [P, 512])
        q_ps = ps("q_ps", [P, 512])

        s = {n: sem("a_" + n) for n in (
            "x_loaded0", "x_loaded1", "src_loaded", "edges_loaded", "params_loaded",
            "bucket_ready", "meta_ready", "counted", "ends_ready", "tails_zeroed",
            "filled", "consts", "v", "pe_setup", "dve_setup", "onehot_ready",
            "carry_ready", "ranks_ready", "ranks_picked", "positions_ready", "stored", "zeros_stored", "stats_waited", "placed_waited",
            "placed", "loaded_tail", "tail_stored",
            "stats_done", "aggregated", "ve_done", "sd_done", "small", "bias_done",
            "h_done", "base_done", "base_stored", "z_done", "lnw_done", "xn_done", "xnt_ps", "xnt_sb", "kv_done", "q_done", "kv_out", "q_out",
            "table_stored", "q_stored")}
        rec_loaded = [sem(f"a_rec_loaded{q}") for q in range(RBUFS)]
        scattered = [sem(f"a_scattered{q}") for q in range(RBUFS)]

        rbf_v = rbf[0:COLS * P, :].rearrange("(p t) f -> p t f", p=P)
        pieces = recs.rearrange("(n s) f -> n (s f)", s=ZROWS)
        NPAR = 16 * 16

        block = st.enter_context(nc.Block())

        @block.sync
        def _(sp):
            sp.wait_ge(s["filled"], 3)
            for to, of, loaded in ((src_i, src, "src_loaded"), (dst_i, dst, "edges_loaded"), (wgt, weight, "edges_loaded")):
                sp.dma_start(to[:, 0:COLS], of[0:COLS * P].rearrange("(p t) -> p t", p=P)).then_inc(s[loaded], 16)
                sp.dma_start(to[0:TAIL, COLS:COLS + 1], of[COLS * P:E].rearrange("(p t) -> p t", t=1)).then_inc(s[loaded], 16)
            for to, of in ((w1s[0:NRBF, :], w1), (w1s[NRBF:NRBF + 1, :], b1.rearrange("(a n) -> a n", a=1)),
                           (w2raw[:], w2.rearrange("(c p) n -> p c n", p=P)), (wos[:], wo.rearrange("(c p) n -> p c n", p=P)),
                           (wqs[:], wq.rearrange("(c p) n -> p c n", p=P)),
                           (wkvs[:, :, 0:H], wk.rearrange("(c p) n -> p c n", p=P)),
                           (wkvs[:, :, H:2 * H], wv.rearrange("(c p) n -> p c n", p=P)),
                           (lnw_b[:], ln_w.partition_broadcast(P)), (lnb_b[:], ln_b.partition_broadcast(P)),
                           (gate_b[:], gate.partition_broadcast(P)),
                           (bias_f[:, 0:H], bq.partition_broadcast(3)), (bias_f[:, H:2 * H], bk.partition_broadcast(3)),
                           (bias_f[:, 2 * H:3 * H], bv.partition_broadcast(3)), (bias_f[:, 3 * H:4 * H], b2.partition_broadcast(3)),
                           (bias_f[:, 4 * H:5 * H], bo.partition_broadcast(3)), (bias_f[:, 5 * H:6 * H], bo.partition_broadcast(3))):
                sp.dma_start(to, of).then_inc(s["params_loaded"], 16)
            sp.wait_ge(s["consts"], 1)
            sp.dma_start(recs[FULL * UNIT:, :].rearrange("(u n s) f -> u n (s f)", n=ZPIECES, s=ZROWS),
                         zero[0:UNITS - FULL, :].unsqueeze(1).to_broadcast([UNITS - FULL, ZPIECES, ZROWS * REC])).then_inc(s["zeros_stored"], 16)
            sp.dma_start(tail_rec[0:TAIL, 0:NRBF], rbf[COLS * P:E, :]).then_inc(s["loaded_tail"], 16)

            def load(g, q, i, first):
                if not first:
                    sp.wait_ge(scattered[q], i * (16 * SCOLS))
                of = rbf_v[:, g * SCOLS:(g + 1) * SCOLS, :] if isinstance(g, int) else rbf_v[:, bass.ds(g * SCOLS, SCOLS), :]
                sp.dma_start(rec[:, q, :, 0:NRBF], of).then_inc(rec_loaded[q], 16)
            for q in range(RBUFS):
                load(q, q, 0, True)
            with sp.Fori(1, RTURNS) as i:
                for q in range(RBUFS):
                    load(i * RBUFS + q, q, i, False)
            for q in range(RREST):
                load(RTURNS * RBUFS + q, q, RTURNS, False)

        @block.gpsimd
        def _(pool):
            pool.memset(src_i[:, COLS:CPAD], NOBUCKET << SHIFT).then_inc(s["filled"], 1)
            pool.memset(dst_i[:, COLS:CPAD], 0).then_inc(s["filled"], 1)
            pool.memset(wgt[:, COLS:CPAD], 0.0).then_inc(s["filled"], 1)
            pool.memset(zero[:, :], 0.0).then_inc(s["consts"], 1)
            pool.memset(ident[:, :], 0.0).then_inc(s["consts"], 1)
            pool.memset(ones_bf[:, :], 1.0).then_inc(s["consts"], 1)
            pool.memset(ones_f[:, :], 1.0).then_inc(s["consts"], 1)
            pool.memset(zero98[:, :], 0.0).then_inc(s["consts"], 1)
            pool.iota(iota1[:, :], [[1, P]], base=1, channel_multiplier=0, allow_small_or_imprecise_dtypes=True).then_inc(s["consts"], 1)
            pool.iota(bucket_ids[:, :], [[1, BUCKETS]], base=0, channel_multiplier=0, allow_small_or_imprecise_dtypes=True).then_inc(s["consts"], 1)
            pool.iota(piece[:, :], [[1, ZPIECES]], base=0, channel_multiplier=0, allow_small_or_imprecise_dtypes=True).then_inc(s["consts"], 1)
            pool.iota(unit_no[:, :], [[1, UNITS]], base=0, channel_multiplier=0, allow_small_or_imprecise_dtypes=True).then_inc(s["consts"], 1)
            pool.wait_ge(s["consts"], 8)
            pool.affine_select(out=ident[:, :], in_=ident[:, :], compare_op=ALU.not_equal, fill=1.0, base=0,
                               pattern=[[-1, P]], channel_multiplier=1).then_inc(s["consts"], 1)
            pool.affine_select(out=tri[:, :], in_=ones_bf[:, :], compare_op=ALU.is_gt, fill=0.0, base=0,
                               pattern=[[1, P]], channel_multiplier=-1).then_inc(s["consts"], 1)
            pool.memset(meta[:, :, 0], 1.0).then_inc(s["meta_ready"], 1)
            pool.wait_ge(s["edges_loaded"], 16 * 4)
            pool.tensor_copy(meta[:, :, 1], wgt[:]).then_inc(s["meta_ready"], 1)
            pool.tensor_copy(meta[:, :, 2], dst_i[:]).then_inc(s["meta_ready"], 1)
            pool.wait_ge(s["zeros_stored"], 16)
            pool.wait_ge(s["ends_ready"], 1)
            for c in range(ZPIECES):
                pool.indirect_dma_start(pieces, bass.IndirectOffsetOnAxis(ap=last_piece[:, c:c + 1], axis=0),
                                        zero[0:BUCKETS, :], None).then_inc(s["tails_zeroed"], 16)
            pool.wait_ge(s["meta_ready"], 4)
            pool.wait_ge(s["tails_zeroed"], 16 * ZPIECES)

            def scatter(g, q, i, pos_wait):
                pool.wait_ge(rec_loaded[q], i * 16 + 16)
                pool.wait_ge(s["positions_ready"], pos_wait)
                pool.tensor_copy(rec[:, q, :, NRBF:REC], meta[:, bass.ds(g * SCOLS, SCOLS), :]).then_inc(s["placed"], 1)
                pool.tensor_copy(slot_i[:, q, :], pos[:, bass.ds(g * SCOLS, SCOLS)]).then_inc(s["placed"], 1)
                pool.wait_ge(s["placed"], g * 2 + 2)
                pool.sem_inc(s["placed_waited"], 1)
                for t in range(SCOLS):
                    pool.indirect_dma_start(recs, bass.IndirectOffsetOnAxis(ap=slot_i[:, q, t:t + 1], axis=0),
                                            rec[:, q, t, :], None).then_inc(scattered[q], 16)
            with pool.Fori(0, RTURNS) as i:
                for q in range(RBUFS):
                    scatter(i * RBUFS + q, q, i, i * (RBUFS * SCOLS // RCOLS) + -(-(q + 1) * SCOLS // RCOLS))
            for q in range(RREST):
                scatter(RTURNS * RBUFS + q, q, RTURNS, RTURNS * (RBUFS * SCOLS // RCOLS) + -(-(q + 1) * SCOLS // RCOLS))
            pool.wait_ge(s["positions_ready"], RGROUPS)
            pool.wait_ge(s["loaded_tail"], 16)
            pool.tensor_copy(tail_rec[0:TAIL, NRBF:REC], meta[0:TAIL, COLS, :]).then_inc(s["placed"], 1)
            pool.tensor_copy(tail_slot[0:TAIL, :], pos[0:TAIL, COLS:COLS + 1]).then_inc(s["placed"], 1)
            pool.wait_ge(s["placed"], 2 * SGROUPS + 2)
            pool.indirect_dma_start(recs, bass.IndirectOffsetOnAxis(ap=tail_slot[0:TAIL, :], axis=0),
                                    tail_rec[0:TAIL, :], None).then_inc(s["tail_stored"], 16)
            pool.wait_ge(s["tail_stored"], 16)
            for q in range(RBUFS):
                pool.wait_ge(scattered[q], 16 * SCOLS * (RTURNS + (q < RREST)))

        @block.vector
        def _(dve):
            steps = [0]

            def link(ins):
                steps[0] += 1
                ins.then_inc(s["v"], 1)
                dve.wait_ge(s["v"], steps[0])

            dve.wait_ge(s["src_loaded"], 32)
            link(dve.tensor_scalar(pos[:], src_i[:], SHIFT, None, ALU.logical_shift_right))
            dve.wait_ge(s["consts"], 11)
            dve.tensor_copy(bucket[:], pos[:]).then_inc(s["bucket_ready"], 1)
            dve.tensor_scalar(cut[:, 0:BUCKETS], bucket_ids[:], -1.0, 0.5, ALU.mult, ALU.add).then_inc(s["bucket_ready"], 1)
            dve.memset(cut[:, BUCKETS:], 0.5 - BUCKETS).then_inc(s["bucket_ready"], 1)
            dve.tensor_copy(bucket_ids_bf[:], bucket_ids[:]).then_inc(s["bucket_ready"], 1)
            dve.wait_ge(s["bucket_ready"], 4)
            def tally(b, q):
                dve.tensor_scalar(eq[:, q, :], bucket[:], bucket_ids[:, bass.ds(b, 1)], 0.0, ALU.is_equal, ALU.add,
                                  accum_out=count[:, bass.ds(b, 1)]).then_inc(s["dve_setup"], 1)
            tally(0, 0)
            tally(1, 1)
            with dve.Fori(1, VBUCKETS // 2) as i:
                for q in range(2):
                    dve.wait_ge(s["dve_setup"], i * 2 + q - 1)
                    tally(i * 2 + q, q)
            dve.wait_ge(s["counted"], BUCKETS + 1 - VBUCKETS)
            link(dve.tensor_tensor(count[:, VBUCKETS:], above[:, VBUCKETS:BUCKETS], above[:, VBUCKETS + 1:], ALU.subtract))
            dve.tensor_scalar(count[:, VBUCKETS:], count[:, VBUCKETS:], 0.5, None, ALU.mult).then_inc(s["dve_setup"], 1)
            dve.wait_ge(s["pe_setup"], 1)
            link(dve.tensor_scalar(units_i[:], setup_ps[:, 0, 0:BUCKETS], float(UNIT - 1), None, ALU.add))
            link(dve.tensor_scalar(units_i[:], units_i[:], USHIFT, None, ALU.logical_shift_right))
            link(dve.tensor_copy(units_f[:], units_i[:]))
            link(dve.tensor_tensor_scan(end_f[:], units_f[:], zero98[:], 0.0, ALU.add, ALU.add))
            link(dve.tensor_tensor(units_f[:], end_f[:], units_f[:], ALU.subtract))
            dve.tensor_scalar(carry[:, 0, :], units_f[:], float(UNIT), None, ALU.mult).then_inc(s["carry_ready"], 1)

            def make_onehot(g, q):
                dve.tensor_tensor(onehot[:, q, :, :], bucket[:, bass.ds(g * RCOLS, RCOLS)].unsqueeze(2).to_broadcast([P, RCOLS, BUCKETS]),
                                  bucket_ids_bf[:].unsqueeze(1).to_broadcast([P, RCOLS, BUCKETS]), ALU.is_equal).then_inc(s["onehot_ready"], 1)

            def pick_ranks(g, q):
                r = rank_ps[:, q, 0:(RCOLS + 1) * BUCKETS].rearrange("p (j b) -> p j b", b=BUCKETS)
                dve.wait_ge(s["ranks_ready"], g + 1)
                dve.tensor_copy(carry[:, 1 - q, :], r[:, RCOLS, :]).then_inc(s["carry_ready"], 1)
                dve.tensor_tensor(ranked[:, q, :, :], r[:, 0:RCOLS, :], onehot[:, q, :, :], ALU.mult).then_inc(s["ranks_picked"], 1)
                dve.wait_ge(s["ranks_picked"], g + 1)
                with nc.allow_low_precision(reason="a slot is one whole number among zeros"):
                    dve.tensor_reduce(pos[:, bass.ds(g * RCOLS, RCOLS)], ranked[:, q, :, :], AX_X, ALU.add).then_inc(s["positions_ready"], 1)

            make_onehot(0, 0)
            dve.wait_ge(s["pe_setup"], 2)
            link(dve.tensor_copy(end_col[:], setup_ps[0:BUCKETS, 1, 0:1]))
            link(dve.tensor_scalar(last_unit[:], end_col[:], float(ZPIECES), -float(ZPIECES), ALU.mult, ALU.add))
            link(dve.tensor_scalar(last_unit[:], last_unit[:], 0.0, None, ALU.max))
            dve.tensor_scalar(last_piece[:], piece[0:BUCKETS, :], last_unit[:, 0:1], None, ALU.add).then_inc(s["ends_ready"], 1)
            link(dve.tensor_scalar(src_i[:], src_i[:], P - 1, None, ALU.bitwise_and))
            dve.tensor_scalar(meta[:, :, 3], src_i[:], -1.0, -1.0, ALU.mult, ALU.add).then_inc(s["meta_ready"], 1)
            with dve.Fori(0, RGROUPS // 2 - 1) as i:
                make_onehot(i * 2 + 1, 1)
                pick_ranks(i * 2, 0)
                make_onehot(i * 2 + 2, 0)
                pick_ranks(i * 2 + 1, 1)
            make_onehot(RGROUPS - 1, 1)
            pick_ranks(RGROUPS - 2, 0)
            pick_ranks(RGROUPS - 1, 1)

            dve.tensor_scalar(unit_no[:], unit_no[:], end_col[:, 0:1], None, ALU.is_ge).then_inc(s["dve_setup"], 1)
            HU = UNITS // 2
            dve.wait_ge(s["pe_setup"], 3)
            for k in range(2):
                dve.tensor_scalar(unit_bucket[:, k * HU:(k + 1) * HU], setup_ps[0:1, k, 0:HU], float(BUCKETS - 1), None, ALU.min)
                dve.tensor_scalar(lagged_bucket[:, LAG + k * HU:LAG + (k + 1) * HU], setup_ps[0:1, k, 0:HU], float(BUCKETS - 1), None, ALU.min)

            dve.memset(lagged_bucket[:, 0:LAG], 0)
            dve.memset(lagged_bucket[:, LAG + UNITS:], 0)

            dve.wait_ge(s["params_loaded"], NPAR)
            dve.tensor_scalar(w2s[:], w2raw[:], 0.5, None, ALU.mult)
            link(dve.tensor_copy(bias_p[:, 0, :], bias_f[:]))
            link(dve.tensor_tensor(bias_r[:], bias_f[:], bias_p[:, 0, :], ALU.subtract))
            link(dve.tensor_copy(bias_p[:, 1, :], bias_r[:]))
            link(dve.tensor_tensor(bias_p[:, 2, :], bias_r[:], bias_p[:, 1, :], ALU.subtract))
            link(dve.tensor_scalar(bias_f[:], bias_p[:, 0, :], ident[0:3, 0:1], None, ALU.mult))
            link(dve.scalar_tensor_tensor(bias_r[:], bias_p[:, 1, :], ident[0:3, 1:2], bias_f[:], ALU.mult, ALU.add))
            dve.scalar_tensor_tensor(bparts[:], bias_p[:, 2, :], ident[0:3, 2:3], bias_r[:], ALU.mult, ALU.add).then_inc(s["bias_done"], 1)

            def normaliser(g, k):
                c = g * 2 + k
                dve.wait_ge(s["aggregated"], c * NG + NG)
                dve.tensor_scalar(ve[:, k, :], mv[:, k, :, 1], EPS, None, ALU.add).then_inc(s["ve_done"], 1)
                dve.wait_ge(s["sd_done"], c + 1)
                dve.reciprocal(rs[:, k, :], sd[:, k, :]).then_inc(s["small"], 1)
                dve.wait_ge(s["small"], c * 6 + 1)
                dve.tensor_tensor(r2[:, k, :], rs[:, k, :], rs[:, k, :], ALU.mult).then_inc(s["small"], 1)
                dve.wait_ge(s["small"], c * 6 + 2)
                dve.tensor_tensor(r2[:, k, :], r2[:, k, :], ve[:, k, :], ALU.mult).then_inc(s["small"], 1)
                dve.wait_ge(s["small"], c * 6 + 3)
                dve.tensor_scalar(r2[:, k, :], r2[:, k, :], -0.5, 1.5, ALU.mult, ALU.add).then_inc(s["small"], 1)
                dve.wait_ge(s["small"], c * 6 + 4)
                dve.tensor_tensor(rs[:, k, :], rs[:, k, :], r2[:, k, :], ALU.mult).then_inc(s["small"], 1)
                dve.wait_ge(s["small"], c * 6 + 5)
                dve.scalar_tensor_tensor(nb[:, k, :], mv[:, k, :, 0], -1.0, rs[:, k, :], ALU.mult, ALU.mult).then_inc(s["small"], 1)

            def statistics(of, k, c):
                for t in range(NG):
                    dve.bn_stats(stats[:, t, :], of[:, t, :]).then_inc(s["stats_done"], 1)
                dve.wait_ge(s["stats_done"], c * NG + NG)
                dve.sem_inc(s["stats_waited"], 1)
                for t in range(NG):
                    dve.bn_aggr(mv[:, k, t, :], stats[:, t, :]).then_inc(s["aggregated"], 1)

            def nodes(g, q, i):
                dve.wait_ge(s[f"x_loaded{q}"], i * 32 + 32)
                statistics(xg[:, q], 0, g * 2)
                normaliser(g, 0)
                dve.wait_ge(s["h_done"], g * NG + NG)
                statistics(hg, 1, g * 2 + 1)
                normaliser(g, 1)
                dve.tensor_tensor(xg[:, q], xg[:, q], hg[:], ALU.add).then_inc(s["base_done"], 1)
                dve.wait_ge(s["z_done"], g * NG + NG)
                dve.tensor_tensor(hg[:], hg[:], lnw_b[:].unsqueeze(1).to_broadcast([P, NG, H]), ALU.mult).then_inc(s["lnw_done"], 1)
                dve.wait_ge(s["lnw_done"], g + 1)

            def xn_of(g):
                dve.tensor_tensor(kvx[:, :, 2 * H:3 * H], hg[:], lnb_b[:].unsqueeze(1).to_broadcast([P, NG, H]), ALU.add).then_inc(s["xn_done"], 1)

            nodes(0, 0, 0)
            xn_of(0)
            nodes(1, 1, 0)
            dve.wait_ge(s["table_stored"], 16)
            xn_of(1)
            with dve.Fori(1, NGROUPS // 2) as i:
                for q in range(2):
                    nodes(i * 2 + q, q, i)
                    dve.wait_ge(s["table_stored"], i * 32 + 16 * q)
                    xn_of(i * 2 + q)

        @block.tensor
        def _(pe):
            pe.wait_ge(s["dve_setup"], VBUCKETS + 1)
            pe.wait_ge(s["consts"], 11)
            pe.matmul(setup_ps[:, 0, 0:BUCKETS], ones_f[:], count[:], start=True, stop=True).then_inc(s["pe_setup"], 1)
            pe.wait_ge(s["carry_ready"], 1)
            pe.transpose(setup_ps[0:BUCKETS, 1, 0:P], end_f[:], ident[:]).then_inc(s["pe_setup"], 1)

            def rank(g, q, reused):
                r = rank_ps[:, q, 0:(RCOLS + 1) * BUCKETS].rearrange("p (j b) -> p j b", b=BUCKETS)
                pe.wait_ge(s["onehot_ready"], g + 1)
                if reused:
                    pe.wait_ge(s["ranks_picked"], g - 1)
                pe.wait_ge(s["carry_ready"], g + 1)
                pe.matmul(r, ident[:], carry[:, q, :].unsqueeze(1).to_broadcast([P, RCOLS + 1, BUCKETS]), start=True, stop=False)
                pe.matmul(r[:, 0:RCOLS, :], tri[:], onehot[:, q, :, :], start=False, stop=False)
                for j in range(RCOLS):
                    n = RCOLS - j
                    m = pe.matmul(r[:, j + 1:RCOLS + 1, :], ones_bf[:], onehot[:, q, j, :].unsqueeze(1).to_broadcast([P, n, BUCKETS]),
                                  start=False, stop=(n == 1))
                m.then_inc(s["ranks_ready"], 1)

            rank(0, 0, False)
            rank(1, 1, False)
            with pe.Fori(1, RGROUPS // 2) as i:
                rank(i * 2, 0, True)
                rank(i * 2 + 1, 1, True)
            HU = UNITS // 2
            pe.wait_ge(s["dve_setup"], VBUCKETS + 2)
            for k in range(2):
                m = pe.matmul(setup_ps[0:1, k, 0:HU], ones_f[0:BUCKETS, 0:1], unit_no[:, k * HU:(k + 1) * HU], start=True, stop=True)
            m.then_inc(s["pe_setup"], 1)

            pe.wait_ge(s["bias_done"], 1)
            pe.wait_ge(s["params_loaded"], NPAR)

            def node_tile(c, g, t, first):
                pe.wait_ge(s["xn_done"], g + 1)
                if not first:
                    pe.wait_ge(s["xnt_sb"], c)
                for k in range(2):
                    m = pe.transpose(t_ps[:, k, :], kvx[:, t, 2 * H + k * P:2 * H + (k + 1) * P], ident[:])
                m.then_inc(s["xnt_ps"], 1)
                pe.wait_ge(s["xnt_sb"], c + 1)
                if not first:
                    pe.wait_ge(s["kv_out"], c)
                pe.matmul(kv_ps[:, 0:2 * H], ones_bf[0:3, :], bparts[:, BKV], start=True, stop=False)
                for k in range(2):
                    m = pe.matmul(kv_ps[:, 0:2 * H], xnT[:, k, :], wkvs[:, k, :], start=False, stop=(k == 1))
                m.then_inc(s["kv_done"], 1)
                if not first:
                    pe.wait_ge(s["q_out"], c)
                pe.matmul(q_ps[:, 0:H], ones_bf[0:3, :], bparts[:, BQ], start=True, stop=False)
                for k in range(2):
                    m = pe.matmul(q_ps[:, 0:H], xnT[:, k, :], wqs[:, k, :], start=False, stop=(k == 1))
                m.then_inc(s["q_done"], 1)

            for t in range(NG):
                node_tile(t, 0, t, t == 0)
            with pe.Fori(1, NGROUPS) as g:
                for t in range(NG):
                    node_tile(g * NG + t, g, t, False)

        @block.scalar
        def _(act):
            def root(c, k):
                act.wait_ge(s["ve_done"], c + 1)
                act.activation(sd[:, k, :], ve[:, k, :], ACT.Sqrt).then_inc(s["sd_done"], 1)

            def node_scalar(g):
                q = g % 2
                root(2 * g, 0)
                act.wait_ge(s["small"], 12 * g + 6)
                if g >= 1:
                    act.wait_ge(s["xn_done"], g)
                for t in range(NG):
                    act.activation(hg[:, t, :], xg[:, q, t, :], ACT.Relu, bias=nb[:, 0, t:t + 1], scale=rs[:, 0, t:t + 1]).then_inc(s["h_done"], 1)
                root(2 * g + 1, 1)
                act.wait_ge(s["small"], 12 * g + 12)
                act.wait_ge(s["base_done"], g + 1)
                act.dma_start(base[g * NG * P:(g + 1) * NG * P, :].rearrange("(t p) f -> p t f", p=P), xg[:, q]).then_inc(s["base_stored"], 16)
                for t in range(NG):
                    act.activation(hg[:, t, :], hg[:, t, :], ACT.Identity, bias=nb[:, 1, t:t + 1], scale=rs[:, 1, t:t + 1]).then_inc(s["z_done"], 1)
                if g + 2 < NGROUPS:
                    act.wait_ge(s["base_stored"], 16 * (g + 1))
                    load_x(g + 2)
                for t in range(NG):
                    c = g * NG + t
                    act.wait_ge(s["xnt_ps"], c + 1)
                    if c >= 1:
                        act.wait_ge(s["q_done"], c)
                    act.activation(xnT[:], t_ps[:], ACT.Copy).then_inc(s["xnt_sb"], 1)
                    act.wait_ge(s["kv_done"], c + 1)
                    act.activation(kvx[:, t, 0:H], kv_ps[:, 0:H], ACT.Copy)
                    act.activation(kvx[:, t, H:2 * H], kv_ps[:, H:2 * H], ACT.Copy, scale=gate_b[:, 0:1]).then_inc(s["kv_out"], 1)
                    act.wait_ge(s["q_done"], c + 1)
                    if t == 0 and g >= 1:
                        act.wait_ge(s["q_stored"], 16 * g)
                    act.activation(qf[:, t, :], q_ps[:, 0:H], ACT.Copy).then_inc(s["q_out"], 1)
                act.wait_ge(s["kv_out"], (g + 1) * NG)
                act.dma_start(table[g * NG * P:(g + 1) * NG * P, :].rearrange("(t p) f -> p t f", p=P), kvx[:]).then_inc(s["table_stored"], 16)
                act.wait_ge(s["q_out"], (g + 1) * NG)
                act.dma_start(queries[g * NG * P:(g + 1) * NG * P, :].rearrange("(t p) f -> p t f", p=P), qf[:]).then_inc(s["q_stored"], 16)

            def load_x(g):
                q = g % 2
                rows = x[g * NG * P:min((g + 1) * NG * P, N), :]
                if g < NGROUPS - 1:
                    half = NG // 2
                    for a, b in ((0, half), (half, NG)):
                        act.dma_start(xg[:, q, a:b, :], rows[a * P:b * P, :].rearrange("(t p) f -> p t f", p=P)).then_inc(s[f"x_loaded{q}"], 16)
                    return
                act.activation(xg[:, q, NG - 1, :], xg[:, q, NG - 1, :], ACT.Copy, scale=0.0).then_inc(s["stored"], 1)
                act.wait_ge(s["stored"], 1)
                act.dma_start(xg[:, q, 0:NG - 1, :], rows[0:(NG - 1) * P, :].rearrange("(t p) f -> p t f", p=P)).then_inc(s[f"x_loaded{q}"], 16)
                act.dma_start(xg[0:LAST_ROWS, q, NG - 1, :], rows[(NG - 1) * P:, :]).then_inc(s[f"x_loaded{q}"], 16)

            act.wait_ge(s["bucket_ready"], 3)
            load_x(0)
            load_x(1)

            def tally(b, q, n):
                if n is not None:
                    act.wait_ge(s["counted"], n)
                scratch = (hg, qf)[q].rearrange("p t f -> p (t f)")[:, 0:CPAD]
                act.activation(scratch, bucket[:], ACT.Sign, bias=cut[:, bass.ds(b, 1)], accum_out=above[:, bass.ds(b, 1)]).then_inc(s["counted"], 1)
            for n in range(3):
                tally(VBUCKETS + n, n % 2, n - 1 if n >= 2 else None)
            with act.Fori(1, (BUCKETS - VBUCKETS) // 2) as i:
                for q in range(2):
                    tally(i * 2 + VBUCKETS + 1 + q, 1 - q, i * 2 + q)
            act.wait_ge(s["counted"], BUCKETS + 1 - VBUCKETS)
            act.wait_ge(s["params_loaded"], NPAR)
            for g in range(NGROUPS):
                node_scalar(g)
            act.wait_ge(s["base_stored"], 16 * NGROUPS)
            act.wait_ge(s["table_stored"], 16 * NGROUPS)
            act.wait_ge(s["q_stored"], 16 * NGROUPS)


def edges(nc, sem, recs, table, queries, ident, ones_bf, iota1, w1s, w2s, bparts, unit_bucket, lagged_bucket, aggr, B2):
    with ExitStack() as st:
        def sb(name, shape, dt=F32):
            return st.enter_context(nc.sbuf_tensor(name, shape, dt))

        def ps(name, shape, dt=F32):
            return st.enter_context(nc.psum_tensor(name, shape, dt))

        rec = sb("urec", [P, DEPTH, 2, REC])
        dst_i = sb("udst", [P, DEPTH, 2], I32)
        qb = sb("uq", [P, DEPTH, H])
        qu = sb("uqupper", [P, QDEPTH, H], I32)
        qs = sb("uqsplit", [P, QDEPTH, 2, H], F32R)
        kvx = sb("ukvx", [P, KVDEPTH, 2, TAB])
        oh = sb("uonehot", [P, OHDEPTH, 2, P])
        away = sb("uaway", [P, 2, 2, P])
        ohb = sb("uonehot_bf", [P, OHBDEPTH, 2, P], BF16)
        ident_bf = sb("ident_bf", [P, P], BF16)
        ohT = sb("uonehotT", [P, 2, 2, P], F32R)
        rT = sb("urT", [NRBF + 1, 2, 2 * P])
        th = sb("utanh", [P, 2, 2, UNIT])
        hid = sb("uhid", [P, 2, 2, UNIT])
        prod = sb("uprod", [P, 2, 2 * NH, HD])
        sc = sb("uscores", [P, 2, 2, NH])
        mx = sb("umax", [P, 2, 2])
        ex = sb("uexp", [P, 2, 2, NH])
        sm = sb("usum", [P, 2, 2])
        rc = sb("urecip", [P, 2, 2])
        av = sb("uav", [P, 2, 2, H])
        phys = sb("uphys", [P, 2, 2, H])
        msg = sb("umsg", [P, MDEPTH, 2, H])
        turn_ps = ps("turn_ps", [P, 4, P])
        hid_ps = [ps(f"hid_ps{k}", [P, 2, UNIT]) for k in range(2)]
        q_ps = ps("uq_ps", [P, 2, H])
        turned_onehots = turn_ps[:, 2, :].bitcast(BF16).rearrange("p (j e) -> p j e", j=2)
        w_ps = [ps(f"w_ps{k}", [P, 2, H]) for k in range(2)]
        ag_ps = [ps(f"ag_ps{k}", [P, 512]) for k in range(2)]

        s = {n: sem("u_" + n) for n in (
            "zeroed", "ident_ready", "q_upper", "q_moved", "q_split", "dst_ready", "dst_waited", "away_ready", "onehot_ready", "turned", "rT_ready", "hid_done", "qe_done", "tanh_ready",
            "hid_ready", "w_done", "qk_done", "scored", "weighted", "max_done", "exp_ready",
            "recip_done", "av_done", "phys_done", "msg_ready", "ag_done", "ag_added")}
        rec_in = [sem(f"u_rec_in{k}") for k in range(DEPTH)]
        q_in = [sem(f"u_q_in{k}") for k in range(DEPTH)]
        kvx_in = [sem(f"u_kvx_in{k}") for k in range(KVDEPTH)]
        TURNS = UNITS // DEPTH
        GATHER_AHEAD, SELECT_AHEAD, SPLIT_AHEAD = 2, 3, 2
        ZSPLIT = 2 * BUCKETS // 5
        rec_v = recs.rearrange("(u p j) f -> u p j f", p=P, j=2)
        q_v = queries.rearrange("(b p) f -> b p f", p=P)

        def turns(eng, body):
            for k in range(DEPTH):
                body(k, k, 0, True, False)
            with eng.Fori(1, TURNS - 1) as i:
                for k in range(DEPTH):
                    body(i * DEPTH + k, k, i, False, False)
            for k in range(DEPTH):
                body((TURNS - 1) * DEPTH + k, k, TURNS - 1, False, True)

        block = st.enter_context(nc.Block())

        @block.sync
        def _(sp):
            bucket_of = [None] * DEPTH

            def unit(u, k, i, first, last):
                if k == 0:
                    _, bucket_of[:] = nc.values_load_multi_w_load_instructions(
                        unit_bucket[0:1, bass.ds(u, DEPTH)], engines=[mybir.EngineType.SP], min_val=0, max_val=BUCKETS - 1)
                if not first:
                    sp.wait_ge(s["av_done"], u - (DEPTH - 1))
                    sp.wait_ge(s["phys_done"], u - (DEPTH - 1))
                sp.dma_start(rec[:, k], rec_v[u] if isinstance(u, int) else rec_v[bass.ds(u, 1)].rearrange("a p j f -> p (a j) f")).then_inc(rec_in[k], 16)
                b = bucket_of[k]
                sp.dma_start(qb[:, k], q_v[bass.ds(b, 1)].rearrange("a p f -> p (a f)")).then_inc(q_in[k], 16)
            turns(sp, unit)

        @block.gpsimd
        def _(pool):
            def gather(u, k, i, first):
                if not (first and k < KVDEPTH):
                    pool.wait_ge(s["av_done"], u - (KVDEPTH - 1))
                    pool.wait_ge(s["phys_done"], u - (KVDEPTH - 1))
                pool.wait_ge(s["dst_ready"], u + 1)
                pool.sem_inc(s["dst_waited"], 1)
                for j in range(2):
                    pool.indirect_dma_start(kvx[:, k % KVDEPTH, j, :], None, table,
                                            bass.IndirectOffsetOnAxis(ap=dst_i[:, k, j:j + 1], axis=0)).then_inc(kvx_in[k % KVDEPTH], 16)

            def sum_up(u, k, i, first):
                q = k % 2
                pool.wait_ge(s["phys_done"], u + 1)
                pool.wait_ge(s["av_done"], u + 1)
                if not (first and k < MDEPTH):
                    pool.wait_ge(s["ag_done"], u - (MDEPTH - 1))
                pool.tensor_tensor(msg[:, k % MDEPTH], phys[:, q], av[:, q], ALU.add).then_inc(s["msg_ready"], 1)

            def split_lower(u, k):
                pool.wait_ge(s["q_upper"], u + 1)
                pool.tensor_tensor(qs[:, k % QDEPTH, 1, :], qb[:, k], qu[:, k % QDEPTH].bitcast(F32), ALU.subtract).then_inc(s["q_split"], 1)

            for k in range(GATHER_AHEAD):
                gather(k, k, 0, True)
                split_lower(k, k)
            pool.memset(aggr[:, 0:ZSPLIT, :], 0.0).then_inc(s["zeroed"], 1)

            def unit(u, k, i, first, last):
                if not (last and k + GATHER_AHEAD >= DEPTH):
                    k2, wrap = (k + GATHER_AHEAD) % DEPTH, (k + GATHER_AHEAD) // DEPTH
                    gather(u + GATHER_AHEAD, k2, i + wrap, first and not wrap)
                if not (last and k + SPLIT_AHEAD >= DEPTH):
                    split_lower(u + SPLIT_AHEAD, (k + SPLIT_AHEAD) % DEPTH)
                if not (first and k < 1):
                    sum_up(u - 1, (k - 1) % DEPTH, i - (k < 1), first)
            turns(pool, unit)
            sum_up(UNITS - 1, DEPTH - 1, TURNS - 1, False)

        @block.scalar
        def _(act):
            def destinations(u, k, i):
                act.wait_ge(rec_in[k], i * 16 + 16)
                act.activation(dst_i[:, k, :], rec[:, k, :, R_DST], ACT.Copy).then_inc(s["dst_ready"], 1)

            def select(u, k, i, first):
                q = k % 2
                act.wait_ge(rec_in[k], i * 16 + 16)
                if not (first and k < OHDEPTH):
                    act.wait_ge(s["ag_done"], u - (OHDEPTH - 1))
                for j in range(2):
                    m = act.activation(away[:, q, j, :], iota1[:], ACT.Abs, bias=rec[:, k, j, R_LOC:R_LOC + 1])
                m.then_inc(s["away_ready"], 1)
                act.wait_ge(s["away_ready"], u + 1)
                if not (first and k < OHBDEPTH):
                    act.wait_ge(s["turned"], u - (OHBDEPTH - 1))
                act.activation(ohb[:, k % OHBDEPTH], away[:, q], ACT.Relu, bias=1.0, scale=-1.0)
                act.activation(oh[:, k % OHDEPTH], away[:, q], ACT.Relu, bias=1.0, scale=-1.0).then_inc(s["onehot_ready"], 1)

            def move_upper(u, k):
                act.wait_ge(s["q_upper"], u + 1)
                act.activation(qs[:, k % QDEPTH, 0, :], qu[:, k % QDEPTH].bitcast(F32), ACT.Copy).then_inc(s["q_moved"], 1)

            def evacuate(u, k, first):
                q = k % 2
                act.wait_ge(s["turned"], u + 1)
                if not (first and k < 2):
                    act.wait_ge(s["qe_done"], u - 1)
                act.activation(rT[:, q, :].rearrange("p (j e) -> p j e", j=2), turn_ps[0:NRBF + 1, 0:2, :], ACT.Copy)
                act.activation(ohT[:, q], turned_onehots, ACT.Copy).then_inc(s["rT_ready"], 1)

            def tanh(u, k, i, first):
                q = k % 2
                act.wait_ge(s["hid_done"], u + 1)
                if not (first and k < 2):
                    act.wait_ge(s["hid_ready"], u - 1)
                act.activation(th[:, q], hid_ps[q][:], ACT.Tanh, scale=0.5).then_inc(s["tanh_ready"], 1)

            def exponent(u, k, i, first):
                q = k % 2
                act.wait_ge(s["max_done"], u + 1)
                if not (first and k < 2):
                    act.wait_ge(s["av_done"], u - 1)
                for j in range(2):
                    m = act.activation(ex[:, q, j, :], sc[:, q, j, :], ACT.Exp, bias=mx[:, q, j:j + 1], accum_out=sm[:, q, j:j + 1])
                m.then_inc(s["exp_ready"], 1)

            act.activation(ident_bf[:], ident[:], ACT.Copy).then_inc(s["ident_ready"], 1)
            for k in range(GATHER_AHEAD):
                destinations(k, k, 0)
            for k in range(SELECT_AHEAD):
                select(k, k, 0, True)
            evacuate(0, 0, True)
            move_upper(0, 0)

            def unit(u, k, i, first, last):
                if not (last and k + 1 >= DEPTH):
                    evacuate(u + 1, (k + 1) % DEPTH, first and k + 1 < DEPTH)
                tanh(u, k, i, first)
                if not (first and k < 1):
                    exponent(u - 1, (k - 1) % DEPTH, i - (k < 1), first and k < 3)
                if not (last and k + GATHER_AHEAD >= DEPTH):
                    destinations(u + GATHER_AHEAD, (k + GATHER_AHEAD) % DEPTH, i + (k + GATHER_AHEAD) // DEPTH)
                if not (last and k + SELECT_AHEAD >= DEPTH):
                    select(u + SELECT_AHEAD, (k + SELECT_AHEAD) % DEPTH, i + (k + SELECT_AHEAD) // DEPTH, first and k + SELECT_AHEAD < DEPTH)
                if not (last and k + 1 >= DEPTH):
                    move_upper(u + 1, (k + 1) % DEPTH)
            turns(act, unit)
            exponent(UNITS - 1, DEPTH - 1, TURNS - 1, False)

        @block.tensor
        def _(pe):
            def turn(u, k, i, first):
                pe.wait_ge(rec_in[k], i * 16 + 16)
                pe.wait_ge(s["onehot_ready"], u + 1)
                if not (first and k < 1):
                    pe.wait_ge(s["rT_ready"], u)
                for j in range(2):
                    pe.transpose(turn_ps[0:NRBF + 1, j, :], rec[:, k, j, 0:NRBF + 1], ident[:])
                for j in range(2):
                    m = pe.transpose(turned_onehots[:, j, :], ohb[:, k % OHBDEPTH, j, :], ident_bf[:])
                m.then_inc(s["turned"], 1)

            def hidden_and_q(u, k, i, first):
                q = k % 2
                pe.wait_ge(s["rT_ready"], u + 1)
                if not (first and k < 2):
                    pe.wait_ge(s["hid_ready"], u - 1)
                for c in range(2):
                    m = pe.matmul(hid_ps[q][:, c, :], w1s[:, c * P:(c + 1) * P], rT[:, q, :], start=(c == 0), stop=True, skip_group_check=True)
                m.then_inc(s["hid_done"], 1)
                pe.wait_ge(s["q_moved"], u + 1)
                pe.wait_ge(s["q_split"], u + 1)
                if not (first and k < 1):
                    pe.wait_ge(s["qk_done"], u)
                for j in range(2):
                    for part in range(2):
                        m = pe.matmul(q_ps[:, j, :], ohT[:, q, j, :], qs[:, k % QDEPTH, part, :], start=(j == 0 and part == 0), stop=(part == 1), skip_group_check=True)
                m.then_inc(s["qe_done"], 1)

            def filters(u, k, i, first):
                q = k % 2
                pe.wait_ge(s["hid_ready"], u + 1)
                if not (first and k < 2):
                    pe.wait_ge(s["phys_done"], u - 1)
                for j in range(2):
                    pe.matmul(w_ps[q][:, j, :], ones_bf[0:3, :], bparts[:, B2], start=(j == 0), stop=False, skip_group_check=True)
                    for c in range(2):
                        m = pe.matmul(w_ps[q][:, j, :], hid[:, q, c, j * P:(j + 1) * P], w2s[:, c, :], start=False, stop=(c == 1), skip_group_check=True)
                m.then_inc(s["w_done"], 1)

            def aggregate(u, k, i, first):
                q = k % 2
                pe.wait_ge(s["msg_ready"], u + 1)
                if not first:
                    pe.wait_ge(s["ag_added"], u - 1)
                for j in range(2):
                    m = pe.matmul(ag_ps[q][:, 0:H], oh[:, k % OHDEPTH, j, :], msg[:, k % MDEPTH, j, :], start=(j == 0), stop=(j == 1))
                m.then_inc(s["ag_done"], 1)

            pe.wait_ge(s["ident_ready"], 1)
            turn(0, 0, 0, True)

            def unit(u, k, i, first, last):
                if not (last and k + 1 >= DEPTH):
                    turn(u + 1, (k + 1) % DEPTH, i + (k + 1) // DEPTH, first and k + 1 < DEPTH)
                hidden_and_q(u, k, i, first)
                if not (first and k < 1):
                    filters(u - 1, (k - 1) % DEPTH, i - (k < 1), first)
                if not (first and k < 3):
                    aggregate(u - 3, (k - 3) % DEPTH, i - (k < 3), first and k < 5)
            turns(pe, unit)
            U = UNITS
            filters(U - 1, DEPTH - 1, TURNS - 1, False)
            aggregate(U - 3, DEPTH - 3, TURNS - 1, False)
            aggregate(U - 2, DEPTH - 2, TURNS - 1, False)
            aggregate(U - 1, DEPTH - 1, TURNS - 1, False)

        @block.vector
        def _(dve):
            dve.memset(aggr[:, ZSPLIT:, :], 0.0).then_inc(s["zeroed"], 1)

            def query_key(u, k, i, first):
                q = k % 2
                dve.wait_ge(s["qe_done"], u + 1)
                dve.wait_ge(kvx_in[k % KVDEPTH], i * (32 * DEPTH // KVDEPTH) + 32 * (k // KVDEPTH + 1))
                if not (first and k < 2):
                    dve.wait_ge(s["scored"], u - 1)
                dve.tensor_tensor(prod[:, q].rearrange("p (j h) d -> p j (h d)", j=2), q_ps[:], kvx[:, k % KVDEPTH, :, 0:H], ALU.mult).then_inc(s["qk_done"], 1)

            def split_upper(u, k, i, first):
                dve.wait_ge(q_in[k], i * 16 + 16)
                if not (first and k < QDEPTH):
                    dve.wait_ge(s["qe_done"], u - (QDEPTH - 1))
                dve.tensor_scalar(qu[:, k % QDEPTH], qb[:, k].bitcast(I32), -4096, None, ALU.bitwise_and).then_inc(s["q_upper"], 1)

            def silu(u, k, i, first):
                q = k % 2
                dve.wait_ge(s["tanh_ready"], u + 1)
                if not (first and k < 2):
                    dve.wait_ge(s["w_done"], u - 1)
                dve.scalar_tensor_tensor(hid[:, q], th[:, q], 1.0, hid_ps[q][:], ALU.add, ALU.mult).then_inc(s["hid_ready"], 1)

            def score(u, k, i, first):
                q = k % 2
                dve.wait_ge(s["qk_done"], u + 1)
                if not (first and k < 2):
                    dve.wait_ge(s["exp_ready"], u - 1)
                dve.tensor_reduce(sc[:, q].rearrange("p j h -> p (j h)"), prod[:, q], AX_X, ALU.add).then_inc(s["scored"], 1)

            def weigh(u, k, i, first):
                q = k % 2
                dve.wait_ge(s["scored"], u + 1)
                dve.scalar_tensor_tensor(sc[:, q], sc[:, q], float(HD) ** -0.5, rec[:, k, :, R_W:R_W + 1].to_broadcast([P, 2, NH]), ALU.mult, ALU.mult).then_inc(s["weighted"], 1)

            def maximum(u, k, i, first):
                q = k % 2
                dve.wait_ge(s["weighted"], u + 1)
                dve.tensor_reduce(mx[:, q], sc[:, q], AX_X, ALU.max, negate=True).then_inc(s["max_done"], 1)

            def invert(u, k, i, first):
                q = k % 2
                dve.wait_ge(s["exp_ready"], u + 1)
                if not (first and k < 2):
                    dve.wait_ge(s["av_done"], u - 1)
                dve.reciprocal(rc[:, q], sm[:, q]).then_inc(s["recip_done"], 1)

            def filtered(u, k, i, first):
                q = k % 2
                dve.wait_ge(s["w_done"], u + 1)
                if not (first and k < 2):
                    dve.wait_ge(s["msg_ready"], u - 1)
                for j in range(2):
                    m = dve.scalar_tensor_tensor(phys[:, q, j, :], w_ps[q][:, j, :], rec[:, k, j, R_W:R_W + 1], kvx[:, k % KVDEPTH, j, 2 * H:3 * H], ALU.mult, ALU.mult)
                m.then_inc(s["phys_done"], 1)

            def attend(u, k, i, first):
                q = k % 2
                dve.wait_ge(s["recip_done"], u + 1)
                if not (first and k < 2):
                    dve.wait_ge(s["msg_ready"], u - 1)
                for j in range(2):
                    m = dve.scalar_tensor_tensor(av[:, q, j, :].rearrange("p (h d) -> p h d", h=NH), kvx[:, k % KVDEPTH, j, H:2 * H].rearrange("p (h d) -> p h d", h=NH),
                                                 rc[:, q, j:j + 1], ex[:, q, j, :].unsqueeze(2).to_broadcast([P, NH, HD]), ALU.mult, ALU.mult)
                m.then_inc(s["av_done"], 1)

            def add_up(u, q, b, first):
                dve.wait_ge(s["ag_done"], u + 1)
                if first:
                    dve.wait_ge(s["zeroed"], 2)
                else:
                    dve.wait_ge(s["ag_added"], u)
                row = aggr[:, bass.ds(b, 1), :].rearrange("p a f -> p (a f)")
                dve.tensor_tensor(row, row, ag_ps[q][:, 0:H], ALU.add).then_inc(s["ag_added"], 1)

            for k in range(SPLIT_AHEAD):
                split_upper(k, k, 0, True)
            bucket_of = [None] * DEPTH

            def unit(u, k, i, first, last):
                if k == 0:
                    _, bucket_of[:] = nc.values_load_multi_w_load_instructions(
                        lagged_bucket[0:1, 0:DEPTH] if first else lagged_bucket[0:1, bass.ds(u, DEPTH)],
                        engines=[mybir.EngineType.DVE], min_val=0, max_val=BUCKETS - 1)
                silu(u, k, i, first)
                query_key(u, k, i, first)
                if not (last and k + SPLIT_AHEAD >= DEPTH):
                    split_upper(u + SPLIT_AHEAD, (k + SPLIT_AHEAD) % DEPTH, i + (k + SPLIT_AHEAD) // DEPTH, first and k + SPLIT_AHEAD < DEPTH)
                if not (first and k < LAG):
                    add_up(u - LAG, (k - LAG) % 2, bucket_of[k], first and k == LAG)
                score(u, k, i, first)
                if not (first and k < 1):
                    before = (u - 1, (k - 1) % DEPTH, i - (k < 1), first)
                    invert(*before)
                weigh(u, k, i, first)
                if not (first and k < 1):
                    filtered(*before)
                maximum(u, k, i, first)
                if not (first and k < 1):
                    attend(*before)
            turns(dve, unit)
            U = UNITS
            before = (U - 1, DEPTH - 1, TURNS - 1, False)
            invert(*before)
            filtered(*before)
            attend(*before)
            _, rest = nc.values_load_multi_w_load_instructions(lagged_bucket[0:1, UNITS:UNITS + DEPTH], engines=[mybir.EngineType.DVE], min_val=0, max_val=BUCKETS - 1)
            for n in range(LAG):
                add_up(U - LAG + n, (U - LAG + n) % 2, rest[n], False)


def finish(nc, sem, base, out, ident, ones_bf, wos, bparts, aggr, BO):
    with ExitStack() as st:
        def sb(name, shape, dt=F32):
            return st.enter_context(nc.sbuf_tensor(name, shape, dt))

        def ps(name, shape, dt=F32):
            return st.enter_context(nc.psum_tensor(name, shape, dt))

        ag = sb("fag", [P, 2, NG, H])
        agT = sb("fagT", [P, 2, 2, P])
        bs = sb("fbase", [P, 2, NG, H])
        ot = sb("fout", [P, 2, NG, H])
        t_ps = [ps(f"ft_ps{k}", [P, 4, P]) for k in range(2)]
        o_ps = [ps(f"fo_ps{k}", [P, 512]) for k in range(2)]
        s = {n: sem("f_" + n) for n in ("copied", "turned", "turned_out", "projected", "summed")}
        base_in = [sem(f"f_base_in{k}") for k in range(2)]
        stored = [sem(f"f_stored{k}") for k in range(2)]
        base_v = base.rearrange("(g t p) f -> g p t f", t=NG, p=P)
        out_v = out[0:(NGROUPS - 1) * NG * P, :].rearrange("(g t p) f -> g p t f", t=NG, p=P)
        PAIRS = NGROUPS // 2
        block = st.enter_context(nc.Block())

        def pairs(eng, body):
            for q in range(2):
                body(q, q, 0, True, False)
            with eng.Fori(1, PAIRS - 1) as i:
                for q in range(2):
                    body(i * 2 + q, q, i, False, False)
            for q in range(2):
                body(NGROUPS - 2 + q, q, PAIRS - 1, False, True)

        @block.sync
        def _(sp):
            def store(g, q):
                sp.wait_ge(s["summed"], g * NG + NG)
                to = out_v[g] if isinstance(g, int) else out_v[bass.ds(g, 1)].rearrange("a p t f -> p (a t) f")
                sp.dma_start(to, ot[:, q]).then_inc(stored[q], 16)

            def group(g, q, i, first, last):
                if not first:
                    store(g - 2, q)
                of = base_v[g] if isinstance(g, int) else base_v[bass.ds(g, 1)].rearrange("a p t f -> p (a t) f")
                sp.dma_start(bs[:, q], of).then_inc(base_in[q], 16)
            pairs(sp, group)
            store(NGROUPS - 2, 0)
            sp.wait_ge(s["summed"], BUCKETS)
            whole = (BUCKETS - 1) * P
            sp.dma_start(out[(NGROUPS - 1) * NG * P:whole, :].rearrange("(t p) f -> p t f", p=P), ot[:, 1, 0:NG - 1, :]).then_inc(stored[1], 16)
            sp.dma_start(out[whole:N, :], ot[0:LAST_ROWS, 1, NG - 1, :]).then_inc(stored[1], 16)
            sp.wait_ge(stored[0], 16 * PAIRS)
            sp.wait_ge(stored[1], 16 * (PAIRS + 1))

        @block.scalar
        def _(act):
            def group(g, q, i, first, last):
                for t in range(NG):
                    b = (q * NG + t) % 2
                    act.wait_ge(s["turned"], g * NG + t + 1)
                    if not (first and q * NG + t < 2):
                        act.wait_ge(s["projected"], g * NG + t - 1)
                    act.activation(agT[:, b], t_ps[b][:, 0:2, :], ACT.Copy).then_inc(s["turned_out"], 1)
            pairs(act, group)

        @block.tensor
        def _(pe):
            def transposed(g, q, t, first):
                b = (q * NG + t) % 2
                if t == 0:
                    pe.wait_ge(s["copied"], g + 1)
                if not (first and q * NG + t < 2):
                    pe.wait_ge(s["turned_out"], g * NG + t - 1)
                for c in range(2):
                    m = pe.transpose(t_ps[b][:, c, :], ag[:, q, t, c * P:(c + 1) * P], ident[:])
                m.then_inc(s["turned"], 1)

            def group(g, q, i, first, last):
                if first and q == 0:
                    transposed(0, 0, 0, True)
                for t in range(NG):
                    b = (q * NG + t) % 2
                    if t + 1 < NG:
                        transposed(g, q, t + 1, first)
                    elif not (last and q == 1):
                        transposed(g + 1, 1 - q, 0, first and q == 0)
                    pe.wait_ge(s["turned_out"], g * NG + t + 1)
                    if not (first and q * NG + t < 2):
                        pe.wait_ge(s["summed"], g * NG + t - 1)
                    pe.matmul(o_ps[b][:, 0:H], ones_bf[0:3, :], bparts[:, BO], start=True, stop=False)
                    for c in range(2):
                        m = pe.matmul(o_ps[b][:, 0:H], agT[:, b, c, :], wos[:, c, :], start=False, stop=(c == 1))
                    m.then_inc(s["projected"], 1)
            pairs(pe, group)

        @block.vector
        def _(dve):
            def copy(g, q, first):
                if not first:
                    dve.wait_ge(s["turned"], g * NG - NG)
                of = aggr[:, g * NG:(g + 1) * NG, :] if isinstance(g, int) else aggr[:, bass.ds(g * NG, NG), :]
                dve.tensor_copy(ag[:, q], of).then_inc(s["copied"], 1)

            def group(g, q, i, first, last):
                if first and q == 0:
                    copy(0, 0, True)
                if not (last and q == 1):
                    copy(g + 1, 1 - q, first and q == 0)
                dve.wait_ge(base_in[q], i * 16 + 16)
                if not first:
                    dve.wait_ge(stored[q], i * 16)
                for t in range(NG):
                    b = (q * NG + t) % 2
                    dve.wait_ge(s["projected"], g * NG + t + 1)
                    dve.tensor_tensor(ot[:, q, t, :], o_ps[b][:, 0:H], bs[:, q, t, :], ALU.add).then_inc(s["summed"], 1)
            pairs(dve, group)


_INS = ["x", "src", "dst", "edge_attr_64", "edge_weight", "L0_gnn_w1", "L0_gnn_b1", "L0_gnn_w2", "L0_gnn_b2", "L0_gnn_ln_w",
        "L0_gnn_ln_b", "L0_gnn_wq", "L0_gnn_bq", "L0_gnn_wk", "L0_gnn_bk", "L0_gnn_wv", "L0_gnn_bv", "L0_gnn_wo", "L0_gnn_bo",
        "L0_gnn_gate"]


def kernel(**inputs):
    import numpy as _np
    import concourse.bacc as _bacc
    from concourse import mybir as _mybir
    from concourse.bass_utils import run_bass_kernel_spmd as _run

    nc = _bacc.Bacc("TRN2", target_bir_lowering=False, num_devices=1)
    arrays, args = {}, []
    for name in _INS:
        a = _np.ascontiguousarray(inputs[name])
        arrays[f"in_{name}"] = a
        args.append(nc.dram_tensor(f"in_{name}", a.shape, _mybir.dt.from_np(a.dtype), kind="ExternalInput").ap())
    args.append(nc.dram_tensor("out", (N, H), F32, kind="ExternalOutput").ap())
    build(nc, *args)
    r = _run(nc, [arrays], core_ids=[0])
    return r.results[0]["out"]
```
